# Optimizing a Trainium2 kernel written in Bass

```python
import numpy as np
import jax
import jax.numpy as jnp

def _softmax(x, axis=-1):
    return jax.nn.softmax(x, axis=axis)

def _gelu(x):
    return jax.nn.gelu(x, approximate=True)

def _silu(x):
    return jax.nn.silu(x)

def _sigmoid(x):
    return jax.nn.sigmoid(x)

def _layernorm(x, axis=-1, eps=1e-05):
    m = jnp.mean(x, axis=axis, keepdims=True)
    v = jnp.var(x, axis=axis, keepdims=True)
    return (x - m) / jnp.sqrt(v + eps)

def _scatter_add(tgt, idx, src, axis=0):
    return tgt.at[idx].add(src)

def _segment_sum(src, seg, n):
    return jax.ops.segment_sum(src, seg, n)
kernel_name = 'mk_adaln_ffn_d2_seqx_r4_d20c35'

def setup_inputs(seed: int=0):
    np.random.seed(seed)
    _w = jnp.asarray

    def _rec_inputs():
        import jax
        import jax.numpy as jnp
        _rk = jax.random.key(seed)
        x = -0.000125 + 0.9999 * jax.random.normal(jax.random.fold_in(_rk, 1), (8, 256, 1024), jnp.float32)
        _lenS = 256 - jax.random.randint(jax.random.fold_in(_rk, 7), (8,), 0, max(1, 256 // 4) + 1, jnp.int32)
        _lenS2 = 256 - jax.random.randint(jax.random.fold_in(_rk, 8), (8,), 0, max(1, 256 // 4) + 1, jnp.int32)
        itok_B_3_7 = jax.random.randint(jax.random.fold_in(_rk, 11), (8,), 3, 8, jnp.int32)
        itok_B_6_15 = jax.random.randint(jax.random.fold_in(_rk, 12), (8,), 6, 16, jnp.int32)
        return (x, itok_B_3_7, itok_B_6_15)
    x, itok_B_3_7, itok_B_6_15 = _rec_inputs()

    def _L0_cond_setup():
        import jax, jax.numpy as jnp
        import numpy as np
        RANK = 16
        ALPHA = 16.0
        SCALING = ALPHA / RANK
        N_ADAPTERS = 8
        IN_F = 1024
        OUT_F = 1024
        BATCH = 4
        SEQ = 512
        key = jax.random.key(seed)
        kx, ka, kb, ki = jax.random.split(key, 4)
        x = jax.random.normal(kx, (BATCH, SEQ, IN_F), dtype=jnp.float32)
        A = jax.random.normal(ka, (N_ADAPTERS, OUT_F, RANK), dtype=jnp.float32) * 0.02
        B = jax.random.normal(kb, (N_ADAPTERS, RANK, IN_F), dtype=jnp.float32) * 0.02
        adapter_ids = jax.random.randint(ki, (BATCH,), 0, N_ADAPTERS, dtype=jnp.int32)
        return {'x': x, 'A': A, 'B': B, 'adapter_ids': adapter_ids}
    _L0_cond_all = _L0_cond_setup()
    _L0_cond_in = {k: v for k, v in _L0_cond_all.items() if k in ('A', 'B')}
    del _L0_cond_all

    def _L0_ffn_setup():
        import jax, jax.numpy as jnp
        import numpy as np
        NUM_EXPERTS = 8
        RANK = 32
        ALPHA = 16.0
        TOP_K = 2
        TEMPERATURE = 1.0
        GAMMA = 0.5
        SOFT_TOPK_TEMP = 0.5
        N_GRAM = 2
        EPS = 1e-06
        key = jax.random.key(seed)
        ks = jax.random.split(key, 6)
        d_in, d_out = (1024, 1024)
        Bsz, T = (4, 512)
        x = jax.random.normal(ks[0], (Bsz, T, d_in), dtype=jnp.float32)
        W = jax.random.normal(ks[1], (d_out, d_in), dtype=jnp.float32) / np.sqrt(d_in)
        b = jax.random.normal(ks[2], (d_out,), dtype=jnp.float32) * 0.01
        A = jax.random.normal(ks[3], (d_in, RANK), dtype=jnp.float32) / np.sqrt(d_in)
        Bmat = jax.random.normal(ks[4], (RANK, d_out), dtype=jnp.float32) * 0.01
        LiMEs = jax.random.normal(ks[5], (NUM_EXPERTS, RANK), dtype=jnp.float32) * 0.1
        return {'x': x, 'W': W, 'b': b, 'A': A, 'Bmat': Bmat, 'LiMEs': LiMEs}
    _L0_ffn_all = _L0_ffn_setup()
    _L0_ffn_in = {k: v for k, v in _L0_ffn_all.items() if k in ('W', 'b', 'A', 'Bmat', 'LiMEs')}
    del _L0_ffn_all

    def _L1_cond_setup():
        import jax, jax.numpy as jnp
        import numpy as np
        B, S, D_IN, D_OUT = (4, 512, 1024, 1024)
        RANK, MAX_LORAS = (16, 32)
        key = jax.random.key(seed)
        ks = jax.random.split(key, 6)
        x = jax.random.normal(ks[0], (B, S, D_IN), dtype=jnp.float32)
        adapter_ids = jax.random.randint(ks[1], (B,), 0, MAX_LORAS)
        base_weight = jax.random.normal(ks[2], (D_OUT, D_IN), dtype=jnp.float32) * D_IN ** (-0.5)
        base_bias = jax.random.normal(ks[3], (D_OUT,), dtype=jnp.float32) * 0.01
        lora_A_w = jax.random.normal(ks[4], (MAX_LORAS, RANK, D_IN), dtype=jnp.float32) * D_IN ** (-0.5)
        lora_B_w = jax.random.normal(ks[5], (MAX_LORAS, D_OUT, RANK), dtype=jnp.float32) * RANK ** (-0.5)
        return {'x': x, 'adapter_ids': adapter_ids, 'base_weight': base_weight, 'base_bias': base_bias, 'lora_A_w': lora_A_w, 'lora_B_w': lora_B_w}
    _L1_cond_all = _L1_cond_setup()
    _L1_cond_in = {k: v for k, v in _L1_cond_all.items() if k in ('base_weight', 'base_bias', 'lora_A_w', 'lora_B_w')}
    del _L1_cond_all

    def _L1_ffn_setup():
        import jax, jax.numpy as jnp
        import numpy as np
        CLIP_RATIO = 1.0
        MAX_QINT = 127.0
        MIN_QINT = -128.0
        key = jax.random.key(seed)
        k1, k2, k3 = jax.random.split(key, 3)
        B, S, IN, OUT = (4, 512, 1024, 1024)
        x = jax.random.normal(k1, (B, S, IN), dtype=jnp.float32)
        weight = jax.random.randint(k2, (OUT, IN), -127, 128, dtype=jnp.int32).astype(jnp.int8)
        weight_scale = jax.random.uniform(k3, (OUT, 1), dtype=jnp.float32) * 0.01 + 0.0001
        return {'x': x, 'weight': weight, 'weight_scale': weight_scale}
    _L1_ffn_all = _L1_ffn_setup()
    _L1_ffn_in = {k: v for k, v in _L1_ffn_all.items() if k in ('weight', 'weight_scale')}
    del _L1_ffn_all
    return {'x': x, 'itok_B_3_7': itok_B_3_7, 'itok_B_6_15': itok_B_6_15, 'L0_cond_A': _L0_cond_in['A'], 'L0_cond_B': _L0_cond_in['B'], 'L0_ffn_W': _L0_ffn_in['W'], 'L0_ffn_b': _L0_ffn_in['b'], 'L0_ffn_A': _L0_ffn_in['A'], 'L0_ffn_Bmat': _L0_ffn_in['Bmat'], 'L0_ffn_LiMEs': _L0_ffn_in['LiMEs'], 'L1_cond_base_weight': _L1_cond_in['base_weight'], 'L1_cond_base_bias': _L1_cond_in['base_bias'], 'L1_cond_lora_A_w': _L1_cond_in['lora_A_w'], 'L1_cond_lora_B_w': _L1_cond_in['lora_B_w'], 'L1_ffn_weight': _L1_ffn_in['weight'], 'L1_ffn_weight_scale': _L1_ffn_in['weight_scale']}

def reference(x, itok_B_3_7, itok_B_6_15, L0_cond_A, L0_cond_B, L0_ffn_W, L0_ffn_b, L0_ffn_A, L0_ffn_Bmat, L0_ffn_LiMEs, L1_cond_base_weight, L1_cond_base_bias, L1_cond_lora_A_w, L1_cond_lora_B_w, L1_ffn_weight, L1_ffn_weight_scale):
    import jax
    import jax.numpy as jnp

    def _L0_cond_ref(x, A, B, adapter_ids):
        import jax, jax.numpy as jnp
        import numpy as np
        RANK = 16
        ALPHA = 16.0
        SCALING = ALPHA / RANK
        N_ADAPTERS = 8
        IN_F = 1024
        OUT_F = 1024
        BATCH = 4
        SEQ = 512
        B_sel = B[adapter_ids]
        A_sel = A[adapter_ids]
        Bx = jnp.einsum('bni,bri->bnr', x, B_sel)
        out = jnp.einsum('bnr,bor->bno', Bx, A_sel)
        return out * SCALING

    def _L0_ffn_ref(x, W, b, A, Bmat, LiMEs):
        import jax, jax.numpy as jnp
        import numpy as np
        NUM_EXPERTS = 8
        RANK = 32
        ALPHA = 16.0
        TOP_K = 2
        TEMPERATURE = 1.0
        GAMMA = 0.5
        SOFT_TOPK_TEMP = 0.5
        N_GRAM = 2
        EPS = 1e-06
        Bsz, T, d_in = x.shape
        E = LiMEs.shape[0]
        scaling = ALPHA / RANK
        H = jnp.einsum('btd,od->bto', x, W) + b
        z = jnp.einsum('btd,dr->btr', x, A)
        anchors = jnp.arange(N_GRAM - 1, T, N_GRAM)
        H_slice = H[:, anchors, :E]
        delta_slice = jnp.einsum('bar,er->bae', z[:, anchors], LiMEs)
        H_scale = jnp.maximum(jnp.max(jnp.abs(H_slice)), EPS)
        d_scale = jnp.maximum(jnp.max(jnp.abs(delta_slice)), EPS)
        logits = ((1.0 - GAMMA) * (H_slice / H_scale) + GAMMA * (delta_slice / d_scale)) / TEMPERATURE
        probs = jax.nn.softmax(logits, axis=-1)
        topk_vals, _ = jax.lax.top_k(probs, TOP_K)
        thresh = topk_vals[..., -1:]
        mask = jax.nn.sigmoid((probs - thresh) / SOFT_TOPK_TEMP)
        weights = probs * mask
        weights = weights / (jnp.sum(weights, axis=-1, keepdims=True) + 1e-09)
        weights_full = jnp.repeat(weights, N_GRAM, axis=1)
        p_mix = jnp.einsum('bte,er->btr', weights_full, LiMEs)
        delta = jnp.einsum('btr,ro->bto', z * p_mix, Bmat) * scaling
        return H + delta

    def _L1_cond_ref(x, adapter_ids, base_weight, base_bias, lora_A_w, lora_B_w):
        import jax, jax.numpy as jnp
        import numpy as np
        B, S, D_IN, D_OUT = (4, 512, 1024, 1024)
        RANK, MAX_LORAS = (16, 32)
        result = jnp.einsum('bsd,od->bso', x, base_weight) + base_bias
        A = lora_A_w[adapter_ids]
        Bw = lora_B_w[adapter_ids]
        h = jnp.einsum('bsd,brd->bsr', x, A)
        lora_out = jnp.einsum('bsr,bor->bso', h, Bw)
        result = result + lora_out
        return result.astype(x.dtype)

    def _L1_ffn_ref(x, weight, weight_scale):
        import jax, jax.numpy as jnp
        import numpy as np
        CLIP_RATIO = 1.0
        MAX_QINT = 127.0
        MIN_QINT = -128.0
        mag = jnp.max(jnp.abs(x), axis=-1, keepdims=True) * CLIP_RATIO
        a_s = jnp.where(mag == 0, 1.0, mag / MAX_QINT)
        a = jnp.clip(jnp.round(x / a_s), MIN_QINT, MAX_QINT).astype(jnp.int8)
        acc = jnp.matmul(a.astype(jnp.int32), weight.T.astype(jnp.int32))
        out = acc.astype(jnp.float32) * a_s * weight_scale.T[None, :, :].reshape(1, 1, -1)
        return out.astype(x.dtype)
    x = x + _L0_ffn_ref(_L0_cond_ref(x, L0_cond_A, L0_cond_B, itok_B_3_7), L0_ffn_W, L0_ffn_b, L0_ffn_A, L0_ffn_Bmat, L0_ffn_LiMEs)
    x = x + _L1_ffn_ref(_L1_cond_ref(x, itok_B_6_15, L1_cond_base_weight, L1_cond_base_bias, L1_cond_lora_A_w, L1_cond_lora_B_w), L1_ffn_weight, L1_ffn_weight_scale)
    return x

_drawn_inputs = setup_inputs


def setup_inputs(seed=0):
    import zlib

    import numpy as np

    out = dict(_drawn_inputs(seed))
    spreads = {}
    factors = {'L0_ffn_b': 4.064,
     'L0_ffn_A': 8.0,
     'L0_ffn_Bmat': 8.0,
     'L0_ffn_LiMEs': 8.0,
     'L1_cond_base_bias': 5.573}
    for name, (base, spread) in spreads.items():
        noise = np.random.default_rng([zlib.crc32(name.encode()), seed]).standard_normal(out[name].shape)
        drawn = base * np.exp(spread * noise) if base else spread * noise
        out[name] = jnp.asarray(drawn.astype(out[name].dtype))
    for name, factor in factors.items():
        out[name] = (out[name] * factor).astype(out[name].dtype)
    return out
```

```python
import concourse.bass as bass
from concourse import mybir
from contextlib import ExitStack

F32 = mybir.dt.float32
F32R = mybir.dt.float32r
BF16 = mybir.dt.bfloat16
I8 = mybir.dt.int8
I32 = mybir.dt.int32
ALU = mybir.AluOpType
ACT = mybir.ActivationFunctionType
AX = mybir.AxisListType

P = 128
NB = 8
D = 1024
KC = D // P
HALF = D // 2
RK = 16
NA0, NA1 = 8, 32
RZ = 32
NE = 8
NT = 2 * NB
NU = RK + RZ
NC = RZ + 2 * NE
NR = NC + RK
U1 = 2 * NU + 2
HR = 2 * RK
U2 = 3 * HR + 2
MAGIC = 1.5 * 2.0 ** 23
QMAX = 127.0
TINY = 2.0 ** -126


def ffn_kernel(nc, x, id0, id1, A0, B0, W0, b0, Affn, Bmat, Lm, Wb, bb, A1, B1, W8, ws, out):
    ctx = ExitStack()
    with ctx:
        def sb(name, shape, dt=F32):
            return ctx.enter_context(nc.sbuf_tensor(name, shape, dt))

        def sem(name):
            return ctx.enter_context(nc.semaphore(name))

        wb_hi = sb("wb_hi", [P, KC, D], F32R)
        wb_lo = sb("wb_lo", [P, KC, D], F32R)
        w8_t = sb("w8_t", [P, KC, D], BF16)
        x_ring = sb("x_ring", [P, 4, D])
        w0_ring = sb("w0_ring", [P, 2, D])
        wb_ring = sb("wb_ring", [P, 2, D])
        w8_bf = sb("w8_bf", [P, 2, D], BF16)
        arena = sb("arena", [P, 4, D])
        bt = sb("bt", [P, KC, NB, 2 * RK], F32R)
        slots = sb("slots", [P, 3 * KC * HR], F32R)
        bt_slot = slots[:, 0:2 * KC * HR].rearrange("p (s k r) -> p s k r", s=2, k=KC)
        a1_b = slots[:, :].rearrange("p (k c r) -> p k c r", k=KC, c=3)
        a1_t = sb("a1_t", [P, NB, KC, 2 * RK], F32R)
        ub = sb("ub", [P, 4, D], F32R)
        u_hi, u_lo = ub[:, 0, :], ub[:, 1, :]
        b1_hi, b1_lo = ub[:, 2, :], ub[:, 3, :]
        right = sb("right", [P, 3, D], F32R)
        upd_hi, upd_lo, lora_r = right[0:U1, 0, :], right[0:NU, 1, :], right[0:U2, 2, :]
        x1t = sb("x1t", [P, 2, D], F32R)
        x1t_both = x1t[:, :, :].rearrange("p s d -> p (s d)").rearrange("p (k c) -> p k c", k=KC)
        x1t_hi, x1t_lo = x1t_both[:, :, 0:P], x1t_both[:, :, P:2 * P]
        xt_hi = [v.rearrange("p s d -> p (s d)").rearrange("p (k c) -> p k c", k=KC) for v in (x1t[:, :, :], ub[:, 0:2, :])]
        xt_lo = [v.rearrange("p s d -> p (s d)").rearrange("p (k c) -> p k c", k=KC)
                 for v in (right[:, 0:2, :], ub[:, 2:4, :])]
        ut = sb("ut", [U1, P], F32R)
        ht = sb("ht", [U2, P], F32R)
        h_sum = sb("h_sum", [3 * HR, P])
        ident = sb("ident", [P, P])
        ident_bf = sb("ident_bf", [P, P], BF16)
        id_sb = sb("id_sb", [1, NB], I32)
        id_bc = sb("id_bc", [P, NB], I32)
        id_f = sb("id_f", [P, NB])
        part = sb("part", [P, 1], I32)
        block_f = sb("block_f", [P, 1])
        onehot = sb("onehot", [P, NB])
        e16 = sb("e16", [P, RK])
        pick = sb("pick", [P, NB, RK])
        pick2 = sb("pick2", [P, NB, 2, RK])
        expand = sb("expand", [RZ + NE, NC])
        p_t = sb("p_t", [RZ + NE, P])
        p_all = sb("p_all", [P, NC])
        p_b = sb("p_b", [2 * RK, NB, NR])
        bx_t = sb("bx_t", [2 * RK, 2, 2 * P])
        z_sb = sb("z_sb", [P, 2, NB, NR])
        l_bc = sb("l_bc", [P, NE, RZ])
        b0_bc = sb("b0_bc", [P, NE])
        amax = sb("amax", [P, 2])
        gmax = sb("gmax", [P, 2])
        ginv = sb("ginv", [P, 2])
        logit = sb("logit", [P, NB, NE])
        prob = sb("prob", [P, NB, NE])
        gate = sb("gate", [P, NB, NE])
        top8 = sb("top8", [P, NB, NE])
        stat = sb("stat", [P, NB])
        pmix = sb("pmix", [P, NB, RZ])
        u_slot = sb("u_slot", [P, 2, U1])
        mag2 = sb("mag2", [P, 2])
        mag = sb("mag", [P, 1])
        a_scale = sb("a_scale", [P, 2])
        a_inv = sb("a_inv", [P, 1])

        early = w8_t[:, :, :].rearrange("p k c -> p (k c)").bitcast(F32)
        a0_k = early[:, 0:D].rearrange("p (k c) -> p k c", k=KC)
        b1_k = early[:, D:2 * D].rearrange("p (k c) -> p k c", k=KC)
        rows = early[:, 2 * D:3 * D]
        m1 = early[:, 3 * D:3 * D + KC * (RZ + NE)].rearrange("p (k c) -> p k c", k=KC)
        split_in = arena[0:RZ + 2, 0, :]
        w0_head = arena[0:NE, 1, :]
        raw_a1, raw_b1 = arena[:, 0, :], arena[:, 1, :]
        ws_bc = arena[:, 0, :]
        u_raw = arena[:, 1, :]
        a0_in = arena[:, 2, :].rearrange("p (b c) -> p b c", b=NB)
        w0t_raw = [arena[:, 2 + s, :] for s in range(2)]
        b1_in = w8_bf[:, :, :].rearrange("p s d -> p (s d)").bitcast(F32).rearrange("p (b c) -> p b c", b=NB)
        split_out = a1_t[0:RZ + 2, :, :, :].rearrange("p b k c -> p (b k c)")
        split_hi, split_lo = split_out[:, 0:D], split_out[:, D:2 * D]
        w8_in8 = wb_ring[:, :, :].rearrange("p s d -> p (s d)").bitcast(I32).rearrange("p (k c) -> p k c", k=KC)
        mixprod = x_ring[:, 2:4, :].rearrange("p s (b r e) -> p (s b) r e", r=RZ, e=NE)
        u_round = x_ring[:, 2, 0:NT * NU].rearrange("p (b j c) -> p b j c", b=NB, j=2).bitcast(F32R)
        u_tok = bt[:, :, :, :].rearrange("p k b r -> p (k b r)")[:, 0:NT * U1].bitcast(F32).rearrange(
            "p (b j c) -> p b j c", b=NB, j=2)
        a_bf = w8_bf[:, 0, :]
        a_t = w8_bf[:, 1, :].rearrange("p (k c) -> p k c", k=KC)
        out_slot = [x_ring[:, 2 + s, :] for s in range(2)]
        x1 = w0_ring
        quant = wb_ring[:, 0, :]
        scaled = wb_ring[:, 1, :]

        def pb(name, shape, dt=F32):
            return ctx.enter_context(nc.psum_tensor(name, shape, dt))

        pA = pb("pA", [P, D])
        pB = pb("pB", [P, D])
        pC = pb("pC", [P, D])
        pD = pb("pD", [P, HALF])
        pE = pb("pE", [P, HALF])
        pA3, pB3, pC3 = (v[:, :].rearrange("p (k c) -> p k c", k=KC) for v in (pA, pB, pC))
        pBh = [pB[:, s * HALF:(s + 1) * HALF].bitcast(BF16) for s in range(2)]
        pDE = [pD, pE]
        pAB = [pA, pB]
        pAB3 = [pA3, pB3]

        b_in, ids_in, head_in, affn_in, a0_loaded, split_loaded, lt_in, bc_in = (
            sem(n) for n in ("b_in", "ids_in", "head_in", "affn_in", "a0_loaded", "split_loaded", "lt_in", "bc_in"))
        id1_in, a1rows_in, b1_loaded = sem("id1_in"), sem("a1rows_in"), sem("b1_loaded")
        masks = sem("masks")
        ones_set = sem("ones_set")
        x_in = [sem(f"x_in{s}") for s in range(4)]
        wb_in = [sem(f"wb_in{s}") for s in range(2)]
        w0_in = [sem(f"w0_in{s}") for s in range(2)]
        w8_in = sem("w8_in")
        chain = sem("chain")
        pick_ready = sem("pick_ready")
        bt_done, bt_high, bt_ready, bt_filled = sem("bt_done"), sem("bt_high"), sem("bt_ready"), sem("bt_filled")
        a0_ordered, b1_ordered = sem("a0_ordered"), sem("b1_ordered")
        p_step, p_copied = sem("p_step"), sem("p_copied")
        split_done = sem("split_done")
        xt_done, xt_high, xt_split = sem("xt_done"), sem("xt_high"), sem("xt_split")
        wbt_done, wb_high, wb_split = sem("wbt_done"), sem("wb_high"), sem("wb_split")
        bxt_done, bxt_copied = sem("bxt_done"), sem("bxt_copied")
        z_done, z_copied = sem("z_done"), sem("z_copied")
        a1t_done, a1_split = sem("a1t_done"), sem("a1_split")
        b1t_done, b1_split = sem("b1t_done"), sem("b1_split")
        raw_ready, lo_ready = sem("raw_ready"), sem("lo_ready")
        w0t_done, w0t_copied = sem("w0t_done"), sem("w0t_copied")
        u_done, u_copied = sem("u_done"), sem("u_copied")
        u_picked, u_split = sem("u_picked"), sem("u_split")
        w8_conv, w8t_done = sem("w8_conv"), sem("w8t_done")
        w8_dve, w8_act = sem("w8_dve"), sem("w8_act")
        const_rows = sem("const_rows")
        ws_in = sem("ws_in")
        amax_ready, gmax_ready = sem("amax_ready"), sem("gmax_ready")
        e1_in, e1_out, e2_in, e2_out = sem("e1_in"), sem("e1_out"), sem("e2_in"), sem("e2_out")
        u_ready = sem("u_ready")
        xm_in = [sem(f"xm_in{s}") for s in range(2)]
        upd_in, lora_in, a1b_ready = sem("upd_in"), sem("lora_in"), sem("a1b_ready")
        slot_ready, slot_used = sem("slot_ready"), sem("slot_used")
        ut_ready = sem("ut_ready")
        x1mm_done, x1_ready, x1_copied = sem("x1mm_done"), sem("x1_ready"), sem("x1_copied")
        x1t_done, hi_ready, x1lo_ready = sem("x1t_done"), sem("hi_ready"), sem("x1lo_ready")
        h_done, h_summed, h_rounded, ht_ready = sem("h_done"), sem("h_summed"), sem("h_rounded"), sem("ht_ready")
        r0_done, r_done = sem("r0_done"), sem("r_done")
        mag_ready, mag1_ready, scale_ready, inv_ready = sem("mag_ready"), sem("mag1_ready"), sem("scale_ready"), sem("inv_ready")
        quant_ready, abf_ready = sem("quant_ready"), sem("abf_ready")
        at_done, at_ready = sem("at_done"), sem("at_ready")
        acc_done, scaled_ready, out_ready = sem("acc_done"), sem("scaled_ready"), sem("out_ready")
        stored = [sem(f"stored{s}") for s in range(2)]

        x_t = x.rearrange("b (p j) d -> b j p d", j=2)
        out_t = out.rearrange("b (p j) d -> b j p d", j=2)
        a0_v = A0.rearrange("a (p k) r -> a p (k r)", p=P)
        b1_v = B1.rearrange("a (p k) r -> a p (k r)", p=P)

        def wait_from(engine, semaphore, count):
            if not isinstance(count, int) or count > 0:
                engine.wait_ge(semaphore, count)

        class Parts:
            def __init__(self, t, b):
                self.cur = not isinstance(t, int) or 0 <= t < NT
                self.prev = not isinstance(t, int) or 0 <= t - 1 < NT
                self.prev2 = not isinstance(t, int) or 0 <= t - 2 < NT
                self.next = not isinstance(t, int) or 0 <= t + 1 < NT

        def main_steps(engine, step):
            step(-1, -1, 1)
            step(0, 0, 0)
            step(1, 0, 1)
            with engine.Fori(1, NB - 1) as b:
                step(b * 2, b, 0)
                step(b * 2 + 1, b, 1)
            step(NT - 2, NB - 1, 0)
            step(NT - 1, NB - 1, 1)
            step(NT, NB, 0)
            step(NT + 1, NB, 1)

        block = ctx.enter_context(nc.Block())

        @block.sync
        def _(sp):
            def move(dst, src):
                return sp.dma_start(dst.bitcast(F32), src.bitcast(F32))

            sp.dma_start(rows, B0.rearrange("a r d -> (a r) d")).then_inc(b_in, 16)

            def load_prepass(q):
                for s in range(4):
                    wait_from(sp, xt_done, q * 4 + (s - 3))
                    sp.dma_start(x_ring[:, s, :], x_t[q * 2 + s // 2, s % 2]).then_inc(x_in[s], 16)
                    if s % 2:
                        wait_from(sp, wbt_done, q * 2 + (s // 2 - 1))
                        sp.dma_start(wb_ring[:, s // 2, :], Wb[bass.ds(q * 2 * P + s // 2 * P, P), :]
                                     ).then_inc(wb_in[s // 2], 16)

            load_prepass(0)
            with sp.Fori(1, NT // 4) as q:
                load_prepass(q)

            def load_weights(q):
                for s in range(2):
                    wait_from(sp, w0t_done, q * 2 + (s - 1))
                    sp.dma_start(w0_ring[:, s, :], W0[bass.ds(q * 2 * P + s * P, P), :]).then_inc(w0_in[s], 16)

            load_weights(0)
            sp.wait_ge(split_done, 1)
            sp.wait_ge(bxt_done, NB)
            for row, src in ((2 * NU, split_hi[RZ:RZ + 1]), (2 * NU + 1, split_lo[RZ:RZ + 1])):
                move(upd_hi[row:row + 1, :], src).then_inc(const_rows, 16)
            for row, src in ((3 * HR, split_hi[RZ + 1:RZ + 2]), (3 * HR + 1, split_lo[RZ + 1:RZ + 2])):
                move(lora_r[row:row + 1, :], src).then_inc(const_rows, 16)
            move(upd_hi[RK:NU, :], split_hi[0:RZ]).then_inc(const_rows, 16)
            move(upd_hi[NU + RK:2 * NU, :], split_hi[0:RZ]).then_inc(const_rows, 16)
            move(upd_lo[RK:NU, :], split_lo[0:RZ]).then_inc(const_rows, 16)
            with sp.Fori(1, KC // 2) as q:
                load_weights(q)
            sp.wait_ge(wbt_done, KC)
            sp.dma_start(w8_in8, W8.rearrange("(k p) c -> p k c", p=P)).then_inc(w8_in, 16)

            def load_x(b, j):
                wait_from(sp, x1_ready, b * 2 + (j - 1))
                sp.dma_start(x_ring[:, j, :], x_t[b, j]).then_inc(xm_in[j], 16)

            def load_update(b):
                wait_from(sp, x1mm_done, b * 2)
                move(upd_hi[0:RK, :], u_hi[b * RK:(b + 1) * RK, :]).then_inc(upd_in, 16)
                move(upd_hi[NU:NU + RK, :], u_hi[b * RK:(b + 1) * RK, :]).then_inc(upd_in, 16)
                move(upd_lo[0:RK, :], u_lo[b * RK:(b + 1) * RK, :]).then_inc(upd_in, 16)

            def load_lora(b):
                wait_from(sp, r_done, b * 2)
                for i, part_of_b1 in enumerate((b1_hi, b1_hi, b1_lo, b1_lo, b1_hi, b1_hi)):
                    move(lora_r[i * RK:(i + 1) * RK, :], part_of_b1[b * RK:(b + 1) * RK, :]).then_inc(lora_in, 16)

            def store(b, j):
                sp.wait_ge(out_ready, b * 2 + (j + 1))
                sp.dma_start(out_t[b, j], out_slot[j]).then_inc(stored[j], 16)

            load_x(0, 0)
            load_x(0, 1)
            sp.wait_ge(lo_ready, 2)
            sp.dma_start(ws_bc, ws.rearrange("n o -> o n").to_broadcast([P, D])).then_inc(ws_in, 16)
            load_lora(0)
            sp.wait_ge(u_split, 2)
            load_update(0)
            load_x(1, 0)
            load_update(1)
            load_x(1, 1)
            load_lora(1)
            for b in range(1, NB - 1):
                load_x(b + 1, 0)
                store(b - 1, 0)
                load_update(b + 1)
                load_x(b + 1, 1)
                store(b - 1, 1)
                load_lora(b + 1)
            for b in (NB - 2, NB - 1):
                for j in range(2):
                    store(b, j)
            sp.wait_ge(stored[0], 16 * NB)
            sp.wait_ge(stored[1], 16 * NB)

        @block.gpsimd
        def _(pool):
            nc.gpsimd.memset(ident[:, :], 0.0).then_inc(masks, 1)
            nc.gpsimd.iota(part[:, :], pattern=[[0, 1]], base=0, channel_multiplier=1).then_inc(masks, 1)
            nc.gpsimd.memset(expand[:, :], 0.0).then_inc(masks, 1)
            nc.gpsimd.memset(ident_bf[:, :], 0.0).then_inc(masks, 1)
            pool.wait_ge(masks, 4)
            nc.gpsimd.affine_select(out=ident[:, :], in_=ident[:, :], compare_op=ALU.not_equal, fill=1.0,
                                    base=0, pattern=[[-1, P]], channel_multiplier=1).then_inc(masks, 1)
            nc.gpsimd.affine_select(out=expand[:, 0:RZ + NE], in_=expand[:, 0:RZ + NE], compare_op=ALU.not_equal,
                                    fill=1.0, base=0, pattern=[[-1, RZ + NE]], channel_multiplier=1
                                    ).then_inc(masks, 1)
            nc.gpsimd.affine_select(out=ident_bf[:, :], in_=ident_bf[:, :], compare_op=ALU.not_equal, fill=1.0,
                                    base=0, pattern=[[-1, P]], channel_multiplier=1).then_inc(masks, 1)
            pool.dma_start(id_sb[0:1, :], id1.rearrange("(o n) -> o n", o=1)).then_inc(id1_in, 16)
            pool.wait_ge(id1_in, 16)
            pool.wait_ge(bt_done, 1)
            for b in range(NB):
                adapter = pool.value_load(id_sb[0:1, b:b + 1], min_val=0, max_val=NA1 - 1)
                pool.dma_start(rows[b * RK:(b + 1) * RK, :],
                               A1[bass.ds(adapter, 1)].rearrange("a r d -> (a r) d")).then_inc(a1rows_in, 16)
                pool.dma_start(b1_in[:, b, :], b1_v[bass.ds(adapter, 1)].rearrange("a p c -> p (a c)")
                               ).then_inc(b1_loaded, 16)

            def fill_bt(b, s):
                wait_from(pool, bxt_done, b - 1)
                nc.gpsimd.tensor_copy(bt_slot[:, s, :, :], bt[:, :, b, :].bitcast(F32)).then_inc(bt_filled, 1)

            pool.wait_ge(bt_ready, 1)
            fill_bt(0, 0)
            fill_bt(1, 1)
            with pool.Fori(1, NB // 2) as q:
                fill_bt(q * 2, 0)
                fill_bt(q * 2 + 1, 1)
            pool.wait_ge(amax_ready, 2)
            nc.gpsimd.partition_all_reduce(gmax[:, :], amax[:, :], P, bass.bass_isa.ReduceOp.max).then_inc(gmax_ready, 1)
            pool.wait_ge(raw_ready, 1)
            nc.gpsimd.tensor_tensor(a1_t[:, :, :, RK:2 * RK].rearrange("p b k r -> p k b r"),
                                    raw_a1.rearrange("p (k b r) -> p k b r", k=KC, b=NB),
                                    a1_t[:, :, :, 0:RK].bitcast(F32).rearrange("p b k r -> p k b r"),
                                    ALU.subtract).then_inc(lo_ready, 1)
            pool.wait_ge(raw_ready, 2)
            nc.gpsimd.tensor_tensor(b1_lo, raw_b1, b1_hi.bitcast(F32), ALU.subtract).then_inc(lo_ready, 1)

            def fill_slot(b, j):
                wait_from(pool, slot_used, b * 2 + (j - 1))
                nc.gpsimd.tensor_copy(u_slot[:, j, :], u_tok[:, b, j, :]).then_inc(slot_ready, 1)

            def fill_a1(b):
                wait_from(pool, h_done, b * 2)
                nc.gpsimd.tensor_copy(a1_b, a1_t[:, bass.ds(b, 1), :, :].bitcast(F32).rearrange("p o k r -> p k o r"
                                      ).to_broadcast([P, KC, 3, HR])).then_inc(a1b_ready, 1)

            pool.wait_ge(lo_ready, 1)
            pool.wait_ge(bxt_done, NB)
            fill_a1(0)
            pool.wait_ge(u_ready, 1)
            fill_slot(0, 0)

            def step(t, b, j):
                go = Parts(t, b)
                if go.prev2:
                    pool.wait_ge(scaled_ready, t - 1)
                    pool.wait_ge(x1_copied, t - 1)
                    nc.gpsimd.tensor_tensor(out_slot[j], scaled, out_slot[j], ALU.add).then_inc(out_ready, 1)
                if not isinstance(t, int) or t + 2 < NT:
                    fill_slot(b + 1, j)
                    if j:
                        fill_a1(b + 1)

            def first_step():
                fill_slot(0, 1)
            first_step()
            step(0, 0, 0)
            step(1, 0, 1)
            with pool.Fori(1, NB - 1) as b:
                step(b * 2, b, 0)
                step(b * 2 + 1, b, 1)
            for t in range(NT - 2, NT + 2):
                step(t, t // 2, t % 2)

        @block.scalar
        def _(act):
            act.dma_start(id_bc[:, :], id0.rearrange("(o n) -> o n", o=1).to_broadcast([P, NB])).then_inc(ids_in, 16)
            act.dma_start(a0_in, a0_v.rearrange("a p c -> p a c")).then_inc(a0_loaded, 16)
            act.dma_start(w0_head, W0[0:NE, :]).then_inc(head_in, 16)
            with nc.allow_non_contiguous_dma(reason="small"):
                act.dma_start(m1[:, :, 0:RZ], Affn.rearrange("(p k) r -> p k r", p=P)).then_inc(affn_in, 16)
                act.dma_start(l_bc[:, :, :].rearrange("p e r -> p (e r)"),
                              Lm.rearrange("(o e) r -> o (e r)", o=1).to_broadcast([P, NE * RZ])).then_inc(bc_in, 16)
                act.dma_start(b0_bc[:, :], b0[0:NE].rearrange("(o e) -> o e", o=1).to_broadcast([P, NE])
                              ).then_inc(bc_in, 16)
                act.wait_ge(masks, 4)
                act.dma_start(expand[0:RZ, RZ + NE:NC], Lm.rearrange("e r -> r e")).then_inc(lt_in, 16)
            act.dma_start(split_in[0:RZ, :], Bmat[:, :]).then_inc(split_loaded, 16)
            act.dma_start(split_in[RZ:RZ + 1, :], b0.rearrange("(o n) -> o n", o=1)).then_inc(split_loaded, 16)
            act.dma_start(split_in[RZ + 1:RZ + 2, :], bb.rearrange("(o n) -> o n", o=1)).then_inc(split_loaded, 16)
            act.wait_ge(bt_done, 1)
            nc.scalar.copy(bt[:, :, :, 0:RK], pC[:, :].rearrange("p (k b r) -> p k b r", k=KC, b=NB)).then_inc(bt_high, 1)

            def prepass(q):
                for i in range(2):
                    b = q * 2 + i
                    for j in range(2):
                        act.wait_ge(xt_done, b * 2 + (j + 1))
                        wait_from(act, bxt_done, b - 1)
                        nc.scalar.copy(xt_hi[i][:, :, j * P:(j + 1) * P], pAB3[j]).then_inc(xt_high, 1)
                    act.wait_ge(wbt_done, b + 1)
                    nc.scalar.copy(wb_hi[:, :, bass.ds(b * P, P)], pC3).then_inc(wb_high, 1)
                    for last, out_of in ((b - 1, 1 - i),):
                        if not isinstance(last, int) or last >= 0:
                            act.wait_ge(bxt_done, last + 1)
                            wait_from(act, z_done, last - 1)
                            nc.scalar.copy(bx_t[:, out_of, :], pD[0:2 * RK, 0:2 * P]).then_inc(bxt_copied, 1)
                    if not isinstance(b, int) or b >= 2:
                        copy_z(b - 2)

            def copy_z(b):
                act.wait_ge(z_done, b + 1)
                nc.scalar.copy(z_sb[:, :, bass.ds(b, 1), :].rearrange("p j o c -> p j (o c)"),
                               pE[:, 0:2 * NR].rearrange("p (j c) -> p j c", j=2)).then_inc(z_copied, 1)

            prepass(0)
            with act.Fori(1, NB // 2) as q:
                prepass(q)
            act.wait_ge(bxt_done, NB)
            nc.scalar.copy(bx_t[:, 1, :], pD[0:2 * RK, 0:2 * P]).then_inc(bxt_copied, 1)
            copy_z(NB - 2)
            copy_z(NB - 1)
            act.wait_ge(b1_loaded, 16 * NB)
            nc.scalar.copy(b1_k.rearrange("p k (b r) -> p k b r", b=NB),
                           b1_in.rearrange("p b (k r) -> p k b r", k=KC)).then_inc(b1_ordered, 1)
            act.wait_ge(a1t_done, 1)
            act.wait_ge(const_rows, 16 * 7)
            a1_src = pA[:, :].rearrange("p (k b r) -> p k b r", k=KC, b=NB)
            nc.scalar.copy(a1_t[:, :, :, 0:RK].rearrange("p b k r -> p k b r"), a1_src).then_inc(a1_split, 1)
            nc.scalar.copy(raw_a1, pA[:, :]).then_inc(raw_ready, 1)
            act.wait_ge(b1t_done, 1)
            nc.scalar.copy(b1_hi.rearrange("m (p k) -> m k p", k=KC), pB3).then_inc(b1_split, 1)
            nc.scalar.copy(raw_b1.rearrange("m (p k) -> m k p", k=KC), pB3).then_inc(raw_ready, 1)

            def softmax_exp():
                act.wait_ge(e1_in, 1)
                nc.scalar.activation(prob[:, :, :], logit[:, :, :], ACT.Exp).then_inc(e1_out, 1)
                act.wait_ge(e2_in, 1)
                nc.scalar.activation(gate[:, :, :], gate[:, :, :], ACT.Exp, scale=-2.0).then_inc(e2_out, 1)

            def weights_tile(q, s):
                act.wait_ge(w0t_done, q * 2 + (s + 1))
                wait_from(act, u_done, q * 2 + (s - 1))
                nc.scalar.copy(w0t_raw[s], pAB[s][:, :]).then_inc(w0t_copied, 1)
                act.wait_ge(u_done, q * 2 + (s + 1))
                if isinstance(q, int) and s == 0:
                    act.wait_ge(lo_ready, 2)
                nc.scalar.copy(u_raw[:, bass.ds(q * 2 * P + s * P, P)], pDE[s][:, 0:P]).then_inc(u_copied, 1)

            weights_tile(0, 0)
            weights_tile(0, 1)
            softmax_exp()
            with act.Fori(1, KC // 2) as q:
                weights_tile(q, 0)
                weights_tile(q, 1)
            act.wait_ge(u_picked, 1)
            nc.scalar.copy(u_hi, pA[:, :]).then_inc(u_split, 1)

            def copy_w8(i):
                act.wait_ge(w8t_done, i * 2 + 2)
                nc.scalar.copy(w8_t[:, :, (i * 2 + 1) * P:(i * 2 + 2) * P],
                               pBh[1].rearrange("p (k c) -> p k c", k=KC)).then_inc(w8_act, 1)

            def step(t, b, j):
                go = Parts(t, b)
                if go.prev:
                    act.wait_ge(quant_ready, t)
                    wait_from(act, at_done, t - 1)
                    nc.scalar.activation(a_bf, quant, ACT.Copy, bias=-MAGIC).then_inc(abf_ready, 1)
                if go.next:
                    act.wait_ge(slot_used, t + 2)
                    wait_from(act, x1mm_done, t + 1)
                    nc.scalar.copy(ut[:, :], pE[0:U1, 0:P]).then_inc(ut_ready, 1)
                if isinstance(t, int) and t == -1:
                    for i in range(KC // 2):
                        copy_w8(i)
                if go.cur:
                    act.wait_ge(h_summed, t + 1)
                    wait_from(act, r_done, t)
                    nc.scalar.copy(ht[0:3 * HR, :], h_sum[:, :]).then_inc(h_rounded, 1)
                if go.prev:
                    act.wait_ge(at_done, t)
                    wait_from(act, acc_done, t - 1)
                    nc.scalar.copy(w8_bf[:, 1, :], pBh[0]).then_inc(at_ready, 1)
                if go.next:
                    act.wait_ge(x1t_done, t + 2)
                    nc.scalar.copy(x1t_hi, pC3).then_inc(hi_ready, 1)
                if go.cur:
                    wait_from(act, stored[j], b * 16)
                    nc.scalar.copy(out_slot[j], x1[:, j, :]).then_inc(x1_copied, 1)

            main_steps(act, step)

        @block.vector
        def _(dve):
            nc.vector.memset(ht[3 * HR:U2, :].bitcast(F32), 1.0).then_inc(ones_set, 1)
            links = [0]

            def link(instruction):
                links[0] += 1
                instruction.then_inc(chain, 1)
                dve.wait_ge(chain, links[0])

            dve.wait_ge(masks, 7)
            link(nc.vector.tensor_scalar(part[:, :], part[:, :], 4, None, ALU.logical_shift_right))
            link(nc.vector.tensor_copy(block_f[:, :], part[:, :]))
            link(nc.vector.tensor_reduce(e16[:, :], ident[:, :].rearrange("p (b r) -> p r b", b=NB), AX.X, ALU.add))
            dve.wait_ge(ids_in, 16)
            link(nc.vector.tensor_copy(id_f[:, :], id_bc[:, :]))
            link(nc.vector.tensor_scalar(onehot[:, :], id_f[:, :], block_f[:, :], None, ALU.is_equal))
            nc.vector.tensor_tensor(pick[:, :, :], onehot[:, :].unsqueeze(2).to_broadcast([P, NB, RK]),
                                    e16[:, :].unsqueeze(1).to_broadcast([P, NB, RK]), ALU.mult).then_inc(pick_ready, 1)
            dve.wait_ge(pick_ready, 1)
            nc.vector.tensor_copy(pick2[:, :, 0, :], pick[:, :, :])
            nc.vector.tensor_copy(pick2[:, :, 1, :], pick[:, :, :]).then_inc(pick_ready, 1)
            nc.vector.tensor_copy(p_b[:, :, NC:NR], e16[0:2 * RK, :].unsqueeze(1).to_broadcast([2 * RK, NB, RK]))
            dve.wait_ge(bt_high, 1)
            nc.vector.tensor_tensor(bt[:, :, :, RK:2 * RK], pC[:, :].rearrange("p (k b r) -> p k b r", k=KC, b=NB),
                                    bt[:, :, :, 0:RK].bitcast(F32), ALU.subtract).then_inc(bt_ready, 1)
            dve.wait_ge(a0_loaded, 16)
            nc.vector.tensor_copy(a0_k.rearrange("p k (b r) -> p k b r", b=NB),
                                  a0_in.rearrange("p b (k r) -> p k b r", k=KC)).then_inc(a0_ordered, 1)

            def split_x(b, i, j):
                dve.wait_ge(xt_high, b * 2 + (j + 1))
                nc.vector.tensor_tensor(xt_lo[i][:, :, j * P:(j + 1) * P], pAB3[j],
                                        xt_hi[i][:, :, j * P:(j + 1) * P].bitcast(F32), ALU.subtract).then_inc(xt_split, 1)

            def split_wb(b):
                dve.wait_ge(wb_high, b + 1)
                nc.vector.tensor_tensor(wb_lo[:, :, bass.ds(b * P, P)], pC3,
                                        wb_hi[:, :, bass.ds(b * P, P)].bitcast(F32), ALU.subtract).then_inc(wb_split, 1)

            split_x(0, 0, 0)
            split_x(0, 0, 1)
            split_wb(0)
            dve.wait_ge(p_step, 1)
            nc.vector.tensor_copy(m1[:, :, RZ:RZ + NE], pE[:, 0:KC * NE].rearrange("p (k e) -> p k e", k=KC)
                                  ).then_inc(p_copied, 1)
            dve.wait_ge(p_step, 2)
            nc.vector.tensor_copy(p_t[:, :], pE[0:RZ + NE, 0:P]).then_inc(p_copied, 1)
            dve.wait_ge(p_step, 3)
            nc.vector.tensor_copy(p_all[:, :], pE[:, 0:NC]).then_inc(p_copied, 1)
            dve.wait_ge(p_step, 4)
            nc.vector.tensor_copy(p_b[:, :, 0:NC], pE[0:2 * RK, 0:NB * NC].rearrange("p (b c) -> p b c", b=NB)
                                  ).then_inc(p_copied, 1)
            split_x(1, 1, 0)
            split_x(1, 1, 1)
            split_wb(1)
            dve.wait_ge(split_loaded, 48)
            link(nc.vector.tensor_copy(split_hi, split_in))
            nc.vector.tensor_tensor(split_lo, split_in, split_hi.bitcast(F32), ALU.subtract).then_inc(split_done, 1)
            with dve.Fori(1, NB // 2) as q:
                for i in range(2):
                    split_x(q * 2 + i, i, 0)
                    split_x(q * 2 + i, i, 1)
                    split_wb(q * 2 + i)
            dve.wait_ge(z_copied, NB)
            dve.wait_ge(bc_in, 32)
            hs, ds_ = z_sb[:, 1, :, RZ:RZ + NE], z_sb[:, 1, :, RZ + NE:NC]
            link(nc.vector.tensor_tensor(hs, hs, b0_bc[:, :].unsqueeze(1).to_broadcast([P, NB, NE]), ALU.add))
            nc.vector.tensor_reduce(amax[:, 0:1], hs, AX.XY, ALU.max, apply_absolute_value=True).then_inc(amax_ready, 1)
            nc.vector.tensor_reduce(amax[:, 1:2], ds_, AX.XY, ALU.max, apply_absolute_value=True).then_inc(amax_ready, 1)
            dve.wait_ge(gmax_ready, 1)
            link(nc.vector.tensor_scalar(gmax[:, :], gmax[:, :], 1e-6, 2.0, ALU.max, ALU.mult))
            link(nc.vector.reciprocal(ginv[:, :], gmax[:, :]))
            link(nc.vector.tensor_scalar(logit[:, :, :], ds_, ginv[:, 1:2], None, ALU.mult))
            link(nc.vector.scalar_tensor_tensor(logit[:, :, :], hs, ginv[:, 0:1], logit[:, :, :], ALU.mult, ALU.add))
            link(nc.vector.tensor_reduce(stat[:, :], logit[:, :, :], AX.X, ALU.max))
            nc.vector.tensor_tensor(logit[:, :, :], logit[:, :, :], stat[:, :].unsqueeze(2).to_broadcast([P, NB, NE]),
                                    ALU.subtract).then_inc(e1_in, 1)
            dve.wait_ge(e1_out, 1)
            link(nc.vector.tensor_reduce(stat[:, :], prob[:, :, :], AX.X, ALU.add))
            link(nc.vector.reciprocal(stat[:, :], stat[:, :]))
            link(nc.vector.tensor_tensor(prob[:, :, :], prob[:, :, :],
                                         stat[:, :].unsqueeze(2).to_broadcast([P, NB, NE]), ALU.mult))
            for b in range(NB):
                last = nc.vector.max(top8[:, b, :], prob[:, b, :])
            link(last)
            nc.vector.tensor_tensor(gate[:, :, :], prob[:, :, :], top8[:, :, 1:2].to_broadcast([P, NB, NE]),
                                    ALU.subtract).then_inc(e2_in, 1)
            dve.wait_ge(e2_out, 1)
            link(nc.vector.tensor_scalar(gate[:, :, :], gate[:, :, :], 1.0, None, ALU.add))
            link(nc.vector.reciprocal(gate[:, :, :], gate[:, :, :]))
            link(nc.vector.tensor_tensor(gate[:, :, :], gate[:, :, :], prob[:, :, :], ALU.mult))
            link(nc.vector.tensor_reduce(stat[:, :], gate[:, :, :], AX.X, ALU.add))
            link(nc.vector.tensor_scalar(stat[:, :], stat[:, :], 1e-9, None, ALU.add))
            link(nc.vector.reciprocal(stat[:, :], stat[:, :]))
            link(nc.vector.tensor_tensor(gate[:, :, :], gate[:, :, :],
                                         stat[:, :].unsqueeze(2).to_broadcast([P, NB, NE]), ALU.mult))
            for b in range(NB):
                last = nc.vector.tensor_tensor(mixprod[:, b, :, :], gate[:, b, :].unsqueeze(1).to_broadcast([P, RZ, NE]),
                                               l_bc[:, :, :].rearrange("p e r -> p r e"), ALU.mult)
            link(last)
            link(nc.vector.tensor_reduce(pmix[:, :, :], mixprod[:, :, :, :], AX.X, ALU.add))
            nc.vector.memset(u_tok[:, :, :, 2 * NU:U1], 1.0).then_inc(ones_set, 1)
            for j in range(2):
                link(nc.vector.scalar_tensor_tensor(u_tok[:, :, j, RK:NU], z_sb[:, j, :, 0:RZ], 0.5, pmix[:, :, :],
                                                    ALU.mult, ALU.mult))
                link(nc.vector.tensor_copy(u_tok[:, :, j, 0:RK], z_sb[:, j, :, NC:NR]))
                link(nc.vector.tensor_copy(u_round[:, :, j, :], u_tok[:, :, j, 0:NU]))
                last = nc.vector.tensor_tensor(u_tok[:, :, j, NU:2 * NU], u_tok[:, :, j, 0:NU],
                                               u_round[:, :, j, :].bitcast(F32), ALU.subtract)
                if j == 0:
                    link(last)
            last.then_inc(u_ready, 1)
            def convert_w8(k):
                wait_from(dve, w8t_done, k - 1)
                nc.vector.tensor_copy(w8_bf[:, k % 2, :], w8_in8[:, k, :].bitcast(I8)).then_inc(w8_conv, 1)

            dve.wait_ge(w8_in, 16)
            dve.wait_ge(b1_ordered, 1)
            convert_w8(0)
            convert_w8(1)
            dve.wait_ge(u_split, 1)
            nc.vector.tensor_tensor(u_lo, pA[:, :], u_hi.bitcast(F32), ALU.subtract).then_inc(u_split, 1)
            for i in range(KC // 2):
                dve.wait_ge(w8t_done, i * 2 + 1)
                nc.vector.tensor_copy(w8_t[:, :, i * 2 * P:(i * 2 + 1) * P],
                                      pBh[0].rearrange("p (k c) -> p k c", k=KC)).then_inc(w8_dve, 1)
                if i < KC // 2 - 1:
                    convert_w8(i * 2 + 2)
                    convert_w8(i * 2 + 3)

            def step(t, b, j):
                go = Parts(t, b)
                nj = 1 - j
                if go.cur:
                    dve.wait_ge(h_done, t + 1)
                    nc.vector.tensor_reduce(h_sum[:, :], pD[0:3 * HR, 0:2 * P].rearrange("m (c t) -> m t c", c=2),
                                            AX.X, ALU.add).then_inc(h_summed, 1)
                    dve.wait_ge(h_rounded, t + 1)
                    low = slice(2 * HR, 3 * HR)
                    nc.vector.tensor_tensor(ht[low, :], h_sum[low, :], ht[low, :].bitcast(F32),
                                            ALU.subtract).then_inc(ht_ready, 1)
                if go.prev2:
                    dve.wait_ge(acc_done, t - 1)
                    wait_from(dve, out_ready, t - 2)
                    nc.vector.scalar_tensor_tensor(scaled, pB[:, :], a_scale[:, j:j + 1], ws_bc,
                                                   ALU.mult, ALU.mult).then_inc(scaled_ready, 1)
                if go.next:
                    dve.wait_ge(x1mm_done, t + 2)
                    dve.wait_ge(xm_in[nj], (b + (1 if j else 0)) * 16 + 16)
                    wait_from(dve, x1_copied, t)
                    nc.vector.tensor_tensor(x1[:, nj, :], pC[:, :], x_ring[:, nj, :], ALU.add).then_inc(x1_ready, 1)
                if go.cur:
                    dve.wait_ge(r0_done, t + 1)
                    nc.vector.tensor_reduce(mag2[:, 0:1], pA[:, 0:HALF], AX.X, ALU.max, apply_absolute_value=True
                                            ).then_inc(mag_ready, 1)
                    dve.wait_ge(r_done, t + 1)
                    nc.vector.tensor_reduce(mag2[:, 1:2], pA[:, HALF:D], AX.X, ALU.max, apply_absolute_value=True
                                            ).then_inc(mag_ready, 1)
                    dve.wait_ge(mag_ready, t * 2 + 2)
                    nc.vector.tensor_tensor(mag[:, :], mag2[:, 0:1], mag2[:, 1:2], ALU.max).then_inc(mag1_ready, 1)
                    dve.wait_ge(mag1_ready, t + 1)
                    nc.vector.tensor_scalar(a_scale[:, j:j + 1], mag[:, :], 1.0 / QMAX, TINY, ALU.mult, ALU.max
                                            ).then_inc(scale_ready, 1)
                    dve.wait_ge(scale_ready, t + 1)
                    nc.vector.reciprocal(a_inv[:, :], a_scale[:, j:j + 1]).then_inc(inv_ready, 1)
                    dve.wait_ge(inv_ready, t + 1)
                    wait_from(dve, abf_ready, t)
                    nc.vector.tensor_scalar(quant, pA[:, :], a_inv[:, :], MAGIC, ALU.mult, ALU.add
                                            ).then_inc(quant_ready, 1)
                if go.next:
                    dve.wait_ge(hi_ready, t + 2)
                    nc.vector.tensor_tensor(x1t_lo, pC3, x1t_hi.bitcast(F32),
                                            ALU.subtract).then_inc(x1lo_ready, 1)

            dve.wait_ge(w0t_done, KC)
            dve.wait_ge(ws_in, 16)
            main_steps(dve, step)

        @block.tensor
        def _(pe):
            pe.wait_ge(masks, 7)
            pe.wait_ge(b_in, 16)
            pe.wait_ge(pick_ready, 1)
            pick_m = pick[:, :, :].rearrange("p b r -> p (b r)")
            for k in range(KC):
                last = nc.tensor.matmul(pC3[:, k, :], rows[:, k * P:(k + 1) * P], pick_m, start=True, stop=True)
            last.then_inc(bt_done, 1)

            def transpose_x(b, i, j):
                s = 2 * i + j
                pe.wait_ge(x_in[s], (b - i) * 8 + 16)
                wait_from(pe, xt_split, b * 2 + (j - 1))
                for k in range(KC):
                    last = nc.tensor.transpose(pAB3[j][:, k, :], x_ring[:, s, k * P:(k + 1) * P], ident[:, :])
                last.then_inc(xt_done, 1)

            def transpose_wb(b, i):
                pe.wait_ge(wb_in[i], (b - i) * 8 + 16)
                wait_from(pe, wb_split, b)
                for k in range(KC):
                    last = nc.tensor.transpose(pC3[:, k, :], wb_ring[:, i, k * P:(k + 1) * P], ident[:, :])
                last.then_inc(wbt_done, 1)

            def project(b, i):
                pe.wait_ge(bt_filled, b + 1)
                pe.wait_ge(xt_split, b * 2 + 2)
                wait_from(pe, bxt_copied, b)
                for k in range(KC):
                    nc.tensor.matmul(pD[0:2 * RK, 0:2 * P], bt_slot[:, i, k, :], xt_hi[i][:, k, :],
                                     start=(k == 0), stop=False)
                    last = nc.tensor.matmul(pD[0:RK, 0:2 * P], bt_slot[:, i, k, 0:RK], xt_lo[i][:, k, :],
                                            start=False, stop=(k == KC - 1))
                last.then_inc(bxt_done, 1)

            def route(b, i):
                pe.wait_ge(bxt_copied, b + 1)
                wait_from(pe, z_copied, b)
                for j in range(2):
                    last = nc.tensor.matmul(pE[:, j * NR:(j + 1) * NR], bx_t[:, i, j * P:(j + 1) * P],
                                            p_b[:, bass.ds(b, 1), :].rearrange("p o c -> p (o c)"),
                                            start=True, stop=True)
                last.then_inc(z_done, 1)

            def prepass(q):
                for i in range(2):
                    b = q * 2 + i
                    transpose_x(b, i, 0)
                    if not isinstance(b, int) or b >= 2:
                        route(b - 2, i)
                    transpose_x(b, i, 1)
                    if isinstance(b, int) and b == 0:
                        pe.wait_ge(bt_ready, 1)
                    transpose_wb(b, i)
                    if not isinstance(b, int) or b >= 1:
                        project(b - 1, 1 - i)
                    if isinstance(b, int) and b == 0:
                        chain_to_p()

            def chain_to_p():
                pe.wait_ge(head_in, 16)
                for k in range(KC):
                    last = nc.tensor.transpose(pE[:, k * NE:(k + 1) * NE], w0_head[:, k:D:KC], ident[0:NE, 0:NE])
                last.then_inc(p_step, 1)
                pe.wait_ge(p_copied, 1)
                pe.wait_ge(affn_in, 16)
                pe.wait_ge(a0_ordered, 1)
                for k in range(KC):
                    last = nc.tensor.matmul(pE[0:RZ + NE, 0:P], m1[:, k, :], a0_k[:, k, :], start=(k == 0), stop=(k == KC - 1))
                last.then_inc(p_step, 1)
                pe.wait_ge(p_copied, 2)
                pe.wait_ge(lt_in, 16)
                nc.tensor.matmul(pE[:, 0:NC], p_t[:, :], expand[:, :], start=True, stop=True).then_inc(p_step, 1)
                pe.wait_ge(p_copied, 3)
                pe.wait_ge(pick_ready, 2)
                for b in range(NB):
                    last = nc.tensor.matmul(pE[0:2 * RK, b * NC:(b + 1) * NC],
                                            pick2[:, b, :, :].rearrange("p h r -> p (h r)"), p_all[:, :],
                                            start=True, stop=True)
                last.then_inc(p_step, 1)
                pe.wait_ge(p_copied, 4)

            prepass(0)
            with pe.Fori(1, NB // 2) as q:
                prepass(q)
            route(NB - 2, 0)
            project(NB - 1, 1)
            route(NB - 1, 1)
            pe.wait_ge(a1rows_in, 16 * NB)
            for k in range(KC):
                last = nc.tensor.transpose(pA3[:, k, :], rows[:, k * P:(k + 1) * P], ident[:, :])
            last.then_inc(a1t_done, 1)
            pe.wait_ge(b1_ordered, 1)
            for k in range(KC):
                last = nc.tensor.transpose(pB3[:, k, :], b1_k[:, k, :], ident[:, :])
            last.then_inc(b1t_done, 1)

            def transpose_w0(q, s):
                pe.wait_ge(w0_in[s], q * 16 + 16)
                wait_from(pe, w0t_copied, q * 2 + (s - 1))
                for k in range(KC):
                    last = nc.tensor.transpose(pAB3[s][:, k, :], w0_ring[:, s, k:D:KC], ident[:, :])
                last.then_inc(w0t_done, 1)

            def apply_w0(q, s):
                pe.wait_ge(w0t_copied, q * 2 + (s + 1))
                wait_from(pe, u_copied, q * 2 + (s - 1))
                for k in range(KC):
                    last = nc.tensor.matmul(pDE[s][:, 0:P], a0_k[:, k, :], w0t_raw[s][:, k * P:(k + 1) * P],
                                            start=(k == 0), stop=(k == KC - 1))
                last.then_inc(u_done, 1)

            pe.wait_ge(raw_ready, 1)
            transpose_w0(0, 0)
            pe.wait_ge(raw_ready, 2)
            transpose_w0(0, 1)
            pe.wait_ge(z_copied, NB)
            apply_w0(0, 0)
            with pe.Fori(1, KC // 2) as q:
                transpose_w0(q, 0)
                apply_w0(q - 1, 1)
                transpose_w0(q, 1)
                apply_w0(q, 0)
            apply_w0(KC // 2 - 1, 1)

            def transpose_w8(i):
                for s in range(2):
                    pe.wait_ge(w8_conv, i * 2 + s + 1)
                    wait_from(pe, (w8_dve, w8_act)[s], i)
                    for k in range(KC):
                        last = nc.tensor.transpose(pBh[s][:, k * P:(k + 1) * P], w8_bf[:, s, k * P:(k + 1) * P],
                                                   ident_bf[:, :])
                    last.then_inc(w8t_done, 1)

            def step(t, b, j):
                go = Parts(t, b)
                nb = b + (1 if j else 0)
                if go.next:
                    pe.wait_ge(slot_ready, t + 2)
                    wait_from(pe, ut_ready, t + 1)
                    nc.tensor.transpose(pE[0:U1, 0:P], u_slot[:, 1 - j, :], ident[:, :]).then_inc(slot_used, 1)
                if isinstance(t, int) and t == -1:
                    for i in range(KC // 2):
                        transpose_w8(i)
                if isinstance(t, int) and t == 0:
                    pe.wait_ge(u_split, 2)
                if go.cur:
                    pe.wait_ge(hi_ready, t + 1)
                    pe.wait_ge(x1lo_ready, t + 1)
                    pe.wait_ge(a1b_ready, b + 1)
                    wait_from(pe, h_summed, t)
                    for k in range(KC):
                        last = nc.tensor.matmul(pD[0:3 * HR, 0:2 * P], a1_b[:, k, :, :].rearrange("p c r -> p (c r)"),
                                                x1t_both[:, k, :], start=(k == 0), stop=(k == KC - 1))
                    last.then_inc(h_done, 1)
                    wait_from(pe, quant_ready, t)

                def product(half):
                    cols = slice(half * HALF, (half + 1) * HALF)
                    for k in range(KC):
                        nc.tensor.matmul(pA[:, cols], x1t_hi[:, k, :], wb_hi[:, k, cols], start=(k == 0), stop=False)
                        nc.tensor.matmul(pA[:, cols], x1t_hi[:, k, :], wb_lo[:, k, cols], start=False, stop=False)
                        nc.tensor.matmul(pA[:, cols], x1t_lo[:, k, :], wb_hi[:, k, cols], start=False, stop=False)

                def lora(half):
                    cols = slice(half * HALF, (half + 1) * HALF)
                    return nc.tensor.matmul(pA[:, cols], ht[:, :], lora_r[:, cols], start=False, stop=True)

                if go.cur:
                    product(0)
                if go.next:
                    pe.wait_ge(ut_ready, t + 2)
                    pe.wait_ge(upd_in, nb * 48 + 48)
                    wait_from(pe, x1lo_ready, t + 1)
                    for half in range(2):
                        cols = slice(half * HALF, (half + 1) * HALF)
                        nc.tensor.matmul(pC[:, cols], ut[:, :], upd_hi[:, cols], start=True, stop=False)
                        last = nc.tensor.matmul(pC[:, cols], ut[0:NU, :], upd_lo[:, cols], start=False, stop=True)
                    last.then_inc(x1mm_done, 1)
                if go.prev:
                    pe.wait_ge(abf_ready, t)
                    wait_from(pe, scaled_ready, t - 1)
                    for k in range(KC):
                        last = nc.tensor.transpose(pBh[0][:, k * P:(k + 1) * P], a_bf[:, k * P:(k + 1) * P], ident_bf[:, :])
                    last.then_inc(at_done, 1)
                if go.cur:
                    pe.wait_ge(ht_ready, t + 1)
                    pe.wait_ge(lora_in, (b + 1) * 16 * 6)
                    lora(0).then_inc(r0_done, 1)
                    product(1)
                    lora(1).then_inc(r_done, 1)
                if go.next:
                    pe.wait_ge(x1_ready, t + 2)
                    for k in range(KC):
                        last = nc.tensor.transpose(pC3[:, k, :], x1[:, 1 - j, k * P:(k + 1) * P], ident[:, :])
                    last.then_inc(x1t_done, 1)
                if go.prev:
                    pe.wait_ge(at_ready, t)
                    for half in range(2):
                        cols = slice(half * HALF, (half + 1) * HALF)
                        for k in range(KC):
                            last = nc.tensor.matmul(pB[:, cols], a_t[:, k, :], w8_t[:, k, cols],
                                                    start=(k == 0), stop=(k == KC - 1))
                    last.then_inc(acc_done, 1)

            pe.wait_ge(u_copied, KC)
            for half in range(2):
                cols = slice(half * HALF, (half + 1) * HALF)
                last = nc.tensor.matmul(pA[:, cols], pick_m, u_raw[:, cols], start=True, stop=True)
            last.then_inc(u_picked, 1)
            pe.wait_ge(wb_split, KC)
            pe.wait_ge(ones_set, 2)
            pe.wait_ge(const_rows, 16 * 7)
            main_steps(pe, step)


_INS = ['x', 'itok_B_3_7', 'itok_B_6_15', 'L0_cond_A', 'L0_cond_B', 'L0_ffn_W', 'L0_ffn_b', 'L0_ffn_A', 'L0_ffn_Bmat',
        'L0_ffn_LiMEs', 'L1_cond_base_weight', 'L1_cond_base_bias', 'L1_cond_lora_A_w', 'L1_cond_lora_B_w',
        'L1_ffn_weight', 'L1_ffn_weight_scale']


def kernel(**inputs):
    import numpy as _np
    import concourse.bacc as _bacc
    from concourse import mybir as _mybir
    from concourse.bass_utils import run_bass_kernel_spmd as _run

    nc = _bacc.Bacc("TRN2", target_bir_lowering=False, num_devices=1)
    arrays, args = {}, []
    for name in _INS:
        a = _np.ascontiguousarray(inputs[name])
        if a.dtype.itemsize == 1:
            a = a.view(_np.int32)
        arrays[f"in_{name}_dram"] = a
        args.append(nc.dram_tensor(f"in_{name}_dram", a.shape, _mybir.dt.from_np(a.dtype), kind="ExternalInput").ap())
    args.append(nc.dram_tensor("out_0_dram", (NB, 2 * P, D), F32, kind="ExternalOutput").ap())
    ffn_kernel(nc, *args)
    r = _run(nc, [arrays], core_ids=[0])
    return r.results[0]["out_0_dram"]
```

```python
import concourse.bass as bass
from concourse import mybir
from contextlib import ExitStack

F32 = mybir.dt.float32
F32R = mybir.dt.float32r
BF16 = mybir.dt.bfloat16
I8 = mybir.dt.int8
I32 = mybir.dt.int32
ALU = mybir.AluOpType
ACT = mybir.ActivationFunctionType
AX = mybir.AxisListType

P = 128
NB = 8
D = 1024
KC = D // P
HALF = D // 2
RK = 16
NA0, NA1 = 8, 32
RZ = 32
NE = 8
NT = 2 * NB
NU = RK + RZ
NC = RZ + 2 * NE
NR = NC + RK
U1 = 2 * NU + 2
HR = 2 * RK
U2 = 3 * HR + 2
MAGIC = 1.5 * 2.0 ** 23
QMAX = 127.0
TINY = 2.0 ** -126


def ffn_kernel(nc, x, id0, id1, A0, B0, W0, b0, Affn, Bmat, Lm, Wb, bb, A1, B1, W8, ws, out):
    ctx = ExitStack()
    with ctx:
        def sb(name, shape, dt=F32):
            return ctx.enter_context(nc.sbuf_tensor(name, shape, dt))

        def sem(name):
            return ctx.enter_context(nc.semaphore(name))

        wb_hi = sb("wb_hi", [P, KC, D], F32R)
        wb_lo = sb("wb_lo", [P, KC, D], F32R)
        w8_t = sb("w8_t", [P, KC, D], BF16)
        x_ring = sb("x_ring", [P, 4, D])
        w0_ring = sb("w0_ring", [P, 2, D])
        wb_ring = sb("wb_ring", [P, 2, D])
        w8_bf = sb("w8_bf", [P, 2, D], BF16)
        arena = sb("arena", [P, 4, D])
        bt = sb("bt", [P, KC, NB, 2 * RK], F32R)
        slots = sb("slots", [P, 3 * KC * HR], F32R)
        bt_slot = slots[:, 0:2 * KC * HR].rearrange("p (s k r) -> p s k r", s=2, k=KC)
        a1_b = slots[:, :].rearrange("p (k c r) -> p k c r", k=KC, c=3)
        a1_t = sb("a1_t", [P, NB, KC, 2 * RK], F32R)
        ub = sb("ub", [P, 4, D], F32R)
        u_hi, u_lo = ub[:, 0, :], ub[:, 1, :]
        b1_hi, b1_lo = ub[:, 2, :], ub[:, 3, :]
        right = sb("right", [P, 3, D], F32R)
        upd_hi, upd_lo, lora_r = right[0:U1, 0, :], right[0:NU, 1, :], right[0:U2, 2, :]
        x1t = sb("x1t", [P, 2, D], F32R)
        x1t_both = x1t[:, :, :].rearrange("p s d -> p (s d)").rearrange("p (k c) -> p k c", k=KC)
        x1t_hi, x1t_lo = x1t_both[:, :, 0:P], x1t_both[:, :, P:2 * P]
        xt_hi = [v.rearrange("p s d -> p (s d)").rearrange("p (k c) -> p k c", k=KC) for v in (x1t[:, :, :], ub[:, 0:2, :])]
        xt_lo = [v.rearrange("p s d -> p (s d)").rearrange("p (k c) -> p k c", k=KC)
                 for v in (right[:, 0:2, :], ub[:, 2:4, :])]
        ut = sb("ut", [U1, P], F32R)
        ht = sb("ht", [U2, P], F32R)
        h_sum = sb("h_sum", [3 * HR, P])
        ident = sb("ident", [P, P])
        ident_bf = sb("ident_bf", [P, P], BF16)
        id_sb = sb("id_sb", [1, 2 * NB], I32)
        id_bc = sb("id_bc", [P, NB], I32)
        id_f = sb("id_f", [P, NB])
        part = sb("part", [P, 1], I32)
        block_f = sb("block_f", [P, 1])
        onehot = sb("onehot", [P, NB])
        e16 = sb("e16", [P, RK])
        pick = sb("pick", [P, NB, RK])
        expand = sb("expand", [RZ + NE, NC])
        p_t = sb("p_t", [RZ + NE, NB, 2, RK])
        p_b = sb("p_b", [2 * RK, NB, NR])
        bx_t = sb("bx_t", [2 * RK, 2, 2 * P])
        z_sb = sb("z_sb", [P, 2, NB, NR])
        l_bc = sb("l_bc", [P, NE, RZ])
        b0_bc = sb("b0_bc", [P, NE])
        amax = sb("amax", [P, 2])
        gmax = sb("gmax", [P, 2])
        ginv = sb("ginv", [P, 2])
        logit = sb("logit", [P, NB, NE])
        prob = sb("prob", [P, NB, NE])
        gate = sb("gate", [P, NB, NE])
        top8 = sb("top8", [P, NB, NE])
        stat = sb("stat", [P, NB])
        pmix = sb("pmix", [P, NB, RZ])
        u_slot = sb("u_slot", [P, 2, U1])
        mag2 = sb("mag2", [P, 2])
        mag = sb("mag", [P, 1])
        a_scale = sb("a_scale", [P, 2])
        a_inv = sb("a_inv", [P, 1])

        early = w8_t[:, :, :].rearrange("p k c -> p (k c)").bitcast(F32)
        a0_k = early[:, 0:D].rearrange("p (k c) -> p k c", k=KC)
        b1_k = early[:, D:2 * D].rearrange("p (k c) -> p k c", k=KC)
        rows = early[:, 2 * D:3 * D]
        m1 = early[:, 3 * D:3 * D + KC * (RZ + NE)].rearrange("p (k c) -> p k c", k=KC)
        split_in = arena[0:RZ + 2, 0, :]
        w0_head = arena[0:NE, 1, :]
        raw_a1, raw_b1 = arena[:, 0, :], x_ring[:, 0, :]
        ws_bc = arena[:, 0, :]
        u_raw = arena[:, 1, :]
        a0_in = arena[:, 2, :].rearrange("p (b c) -> p b c", b=NB)
        w0t_raw = [arena[:, 2 + s, :] for s in range(2)]
        b1_in = w8_bf[:, :, :].rearrange("p s d -> p (s d)").bitcast(F32).rearrange("p (b c) -> p b c", b=NB)
        split_out = a1_t[0:RZ + 2, :, :, :].rearrange("p b k c -> p (b k c)")
        split_hi, split_lo = split_out[:, 0:D], split_out[:, D:2 * D]
        w8_in8 = wb_ring[:, :, :].rearrange("p s d -> p (s d)").bitcast(I32).rearrange("p (k c) -> p k c", k=KC)
        w8_tile = [v.bitcast(BF16)[:, h * D:(h + 1) * D] if v is not None else w8_bf[:, h, :]
                   for v in (None, x_ring[:, 1, :], x_ring[:, 2, :], x_ring[:, 3, :]) for h in range(2)]
        mixprod = x_ring[:, 2:4, :].rearrange("p s (b r e) -> p (s b) r e", r=RZ, e=NE)
        u_round = x_ring[:, 2, 0:NT * NU].rearrange("p (b j c) -> p b j c", b=NB, j=2).bitcast(F32R)
        u_tok = bt[:, :, :, :].rearrange("p k b r -> p (k b r)")[:, 0:NT * U1].bitcast(F32).rearrange(
            "p (b j c) -> p b j c", b=NB, j=2)
        a_bf = w8_bf[:, 0, :]
        a_t = w8_bf[:, 1, :].rearrange("p (k c) -> p k c", k=KC)
        out_slot = [x_ring[:, 2 + s, :] for s in range(2)]
        x1 = w0_ring
        quant = wb_ring[:, 0, :]
        scaled = wb_ring[:, 1, :]

        def pb(name, shape, dt=F32):
            return ctx.enter_context(nc.psum_tensor(name, shape, dt))

        pA = pb("pA", [P, D])
        pB = pb("pB", [P, D])
        pC = pb("pC", [P, D])
        pD = pb("pD", [P, HALF])
        pE = pb("pE", [P, HALF])
        pA3, pB3, pC3 = (v[:, :].rearrange("p (k c) -> p k c", k=KC) for v in (pA, pB, pC))
        pABh = [v[:, s * HALF:(s + 1) * HALF].bitcast(BF16) for v in (pA, pB) for s in range(2)]
        pBh = pABh[2:]
        pDE = [pD, pE]
        pAB = [pA, pB]
        pAB3 = [pA3, pB3]

        b_in, ids_in, id0_in, head_in, affn_in, a0_loaded, split_loaded, lt_in, bc_in = (
            sem(n) for n in ("b_in", "ids_in", "id0_in", "head_in", "affn_in", "a0_loaded", "split_loaded", "lt_in", "bc_in"))
        id1_in, a1rows_in, b1_loaded = sem("id1_in"), sem("a1rows_in"), sem("b1_loaded")
        masks = sem("masks")
        ones_set = sem("ones_set")
        x_in = [sem(f"x_in{s}") for s in range(4)]
        wb_in = [sem(f"wb_in{s}") for s in range(2)]
        w0_in = [sem(f"w0_in{s}") for s in range(2)]
        w8_in = sem("w8_in")
        chain = sem("chain")
        pick_ready = sem("pick_ready")
        bt_done, bt_high, bt_ready, bt_filled = sem("bt_done"), sem("bt_high"), sem("bt_ready"), sem("bt_filled")
        a0_ordered, b1_ordered = sem("a0_ordered"), sem("b1_ordered")
        p_through = sem("p_through")
        p_step, p_copied = sem("p_step"), sem("p_copied")
        split_done = sem("split_done")
        xt_done, xt_high, xt_split = sem("xt_done"), sem("xt_high"), sem("xt_split")
        wbt_done, wb_high, wb_split = sem("wbt_done"), sem("wb_high"), sem("wb_split")
        bxt_done, bxt_copied = sem("bxt_done"), sem("bxt_copied")
        z_done, z_copied = sem("z_done"), sem("z_copied")
        a1t_done, a1_split = sem("a1t_done"), sem("a1_split")
        b1t_done, b1_split = sem("b1t_done"), sem("b1_split")
        raw_ready, lo_ready = sem("raw_ready"), sem("lo_ready")
        w0t_done, w0t_copied = sem("w0t_done"), sem("w0t_copied")
        u_done, u_copied = sem("u_done"), sem("u_copied")
        u_split = sem("u_split")
        w8_conv, w8t_done = sem("w8_conv"), sem("w8t_done")
        w8_dve, w8_act = sem("w8_dve"), sem("w8_act")
        const_rows = sem("const_rows")
        ws_in = sem("ws_in")
        amax_ready, gmax_ready = sem("amax_ready"), sem("gmax_ready")
        e1_in, e1_out, e2_in, e2_out = sem("e1_in"), sem("e1_out"), sem("e2_in"), sem("e2_out")
        u_ready = sem("u_ready")
        xm_in = [sem(f"xm_in{s}") for s in range(2)]
        upd_in, lora_in, a1b_ready = sem("upd_in"), sem("lora_in"), sem("a1b_ready")
        slot_ready, slot_used = sem("slot_ready"), sem("slot_used")
        ut_ready = sem("ut_ready")
        x1mm_done, x1_ready, x1_copied = sem("x1mm_done"), sem("x1_ready"), sem("x1_copied")
        x1t_done, hi_ready, x1lo_ready = sem("x1t_done"), sem("hi_ready"), sem("x1lo_ready")
        h_done, h_summed, h_rounded, ht_ready = sem("h_done"), sem("h_summed"), sem("h_rounded"), sem("ht_ready")
        r0_done, r_done = sem("r0_done"), sem("r_done")
        mag_ready, mag1_ready, scale_ready, inv_ready = sem("mag_ready"), sem("mag1_ready"), sem("scale_ready"), sem("inv_ready")
        quant_ready, abf_ready = sem("quant_ready"), sem("abf_ready")
        at_done, at_ready = sem("at_done"), sem("at_ready")
        acc_done, scaled_ready, out_ready = sem("acc_done"), sem("scaled_ready"), sem("out_ready")
        stored = [sem(f"stored{s}") for s in range(2)]

        x_t = x.rearrange("b (p j) d -> b j p d", j=2)
        out_t = out.rearrange("b (p j) d -> b j p d", j=2)
        a0_v = A0.rearrange("a (p k) r -> a p (k r)", p=P)
        b1_v = B1.rearrange("a (p k) r -> a p (k r)", p=P)

        def wait_from(engine, semaphore, count):
            if not isinstance(count, int) or count > 0:
                engine.wait_ge(semaphore, count)

        class Parts:
            def __init__(self, t, b):
                self.cur = not isinstance(t, int) or 0 <= t < NT
                self.prev = not isinstance(t, int) or 0 <= t - 1 < NT
                self.prev2 = not isinstance(t, int) or 0 <= t - 2 < NT
                self.next = not isinstance(t, int) or 0 <= t + 1 < NT

        def main_steps(engine, step):
            step(-1, -1, 1)
            step(0, 0, 0)
            step(1, 0, 1)
            with engine.Fori(1, NB - 1) as b:
                step(b * 2, b, 0)
                step(b * 2 + 1, b, 1)
            step(NT - 2, NB - 1, 0)
            step(NT - 1, NB - 1, 1)
            step(NT, NB, 0)
            step(NT + 1, NB, 1)

        block = ctx.enter_context(nc.Block())

        @block.sync
        def _(sp):
            def move(dst, src):
                return sp.dma_start(dst.bitcast(F32), src.bitcast(F32))

            sp.dma_start(rows, B0.rearrange("a r d -> (a r) d")).then_inc(b_in, 16)

            def load_prepass(q):
                for s in range(4):
                    wait_from(sp, xt_done, q * 4 + (s - 3))
                    sp.dma_start(x_ring[:, s, :], x_t[q * 2 + s // 2, s % 2]).then_inc(x_in[s], 16)
                    if s % 2:
                        wait_from(sp, wbt_done, q * 2 + (s // 2 - 1))
                        sp.dma_start(wb_ring[:, s // 2, :], Wb[bass.ds(q * 2 * P + s // 2 * P, P), :]
                                     ).then_inc(wb_in[s // 2], 16)

            load_prepass(0)
            sp.wait_ge(id0_in, 16)
            for b in range(NB):
                adapter = sp.value_load(id_sb[0:1, b:b + 1], min_val=0, max_val=NA0 - 1)
                sp.dma_start(a0_in[:, b, :], a0_v[bass.ds(adapter, 1)].rearrange("a p c -> p (a c)")
                             ).then_inc(a0_loaded, 16)
            with sp.Fori(1, NT // 4) as q:
                load_prepass(q)

            def load_weights(q):
                for s in range(2):
                    wait_from(sp, w0t_done, q * 2 + (s - 1))
                    sp.dma_start(w0_ring[:, s, :], W0[bass.ds(q * 2 * P + s * P, P), :]).then_inc(w0_in[s], 16)

            load_weights(0)
            sp.wait_ge(wbt_done, KC)
            sp.dma_start(w8_in8, W8.rearrange("(k p) c -> p k c", p=P)).then_inc(w8_in, 16)
            sp.wait_ge(split_done, 1)
            sp.wait_ge(bxt_done, NB - 1)
            for row, src in ((2 * NU, split_hi[RZ:RZ + 1]), (2 * NU + 1, split_lo[RZ:RZ + 1])):
                move(upd_hi[row:row + 1, :], src).then_inc(const_rows, 16)
            for row, src in ((3 * HR, split_hi[RZ + 1:RZ + 2]), (3 * HR + 1, split_lo[RZ + 1:RZ + 2])):
                move(lora_r[row:row + 1, :], src).then_inc(const_rows, 16)
            move(upd_hi[RK:NU, :], split_hi[0:RZ]).then_inc(const_rows, 16)
            move(upd_hi[NU + RK:2 * NU, :], split_hi[0:RZ]).then_inc(const_rows, 16)
            move(upd_lo[RK:NU, :], split_lo[0:RZ]).then_inc(const_rows, 16)
            with sp.Fori(1, KC // 2) as q:
                load_weights(q)

            def load_x(b, j):
                wait_from(sp, x1_ready, b * 2 + (j - 1))
                sp.dma_start(x_ring[:, j, :], x_t[b, j]).then_inc(xm_in[j], 16)

            def load_update(b):
                wait_from(sp, x1mm_done, b * 2)
                move(upd_hi[0:RK, :], u_hi[b * RK:(b + 1) * RK, :]).then_inc(upd_in, 16)
                move(upd_hi[NU:NU + RK, :], u_hi[b * RK:(b + 1) * RK, :]).then_inc(upd_in, 16)
                move(upd_lo[0:RK, :], u_lo[b * RK:(b + 1) * RK, :]).then_inc(upd_in, 16)

            def load_lora(b):
                wait_from(sp, r_done, b * 2)
                for i, part_of_b1 in enumerate((b1_hi, b1_hi, b1_lo, b1_lo, b1_hi, b1_hi)):
                    move(lora_r[i * RK:(i + 1) * RK, :], part_of_b1[b * RK:(b + 1) * RK, :]).then_inc(lora_in, 16)

            def store(b, j):
                sp.wait_ge(out_ready, b * 2 + (j + 1))
                sp.dma_start(out_t[b, j], out_slot[j]).then_inc(stored[j], 16)

            sp.wait_ge(lo_ready, 2)
            sp.dma_start(ws_bc, ws.rearrange("n o -> o n").to_broadcast([P, D])).then_inc(ws_in, 16)
            load_x(0, 0)
            load_lora(0)
            sp.wait_ge(u_split, KC)
            load_update(0)
            sp.wait_ge(w8t_done, 4)
            load_x(0, 1)
            load_x(1, 0)
            load_update(1)
            load_x(1, 1)
            load_lora(1)
            for b in range(1, NB - 1):
                load_x(b + 1, 0)
                store(b - 1, 0)
                load_update(b + 1)
                load_x(b + 1, 1)
                store(b - 1, 1)
                load_lora(b + 1)
            for b in (NB - 2, NB - 1):
                for j in range(2):
                    store(b, j)
            sp.wait_ge(stored[0], 16 * NB)
            sp.wait_ge(stored[1], 16 * NB)

        @block.gpsimd
        def _(pool):
            nc.gpsimd.memset(ident[:, :], 0.0).then_inc(masks, 1)
            nc.gpsimd.iota(part[:, :], pattern=[[0, 1]], base=0, channel_multiplier=1).then_inc(masks, 1)
            nc.gpsimd.memset(expand[:, :], 0.0).then_inc(masks, 1)
            nc.gpsimd.memset(ident_bf[:, :], 0.0).then_inc(masks, 1)
            pool.wait_ge(masks, 4)
            nc.gpsimd.affine_select(out=ident[:, :], in_=ident[:, :], compare_op=ALU.not_equal, fill=1.0,
                                    base=0, pattern=[[-1, P]], channel_multiplier=1).then_inc(masks, 1)
            nc.gpsimd.affine_select(out=expand[:, 0:RZ + NE], in_=expand[:, 0:RZ + NE], compare_op=ALU.not_equal,
                                    fill=1.0, base=0, pattern=[[-1, RZ + NE]], channel_multiplier=1
                                    ).then_inc(masks, 1)
            nc.gpsimd.affine_select(out=ident_bf[:, :], in_=ident_bf[:, :], compare_op=ALU.not_equal, fill=1.0,
                                    base=0, pattern=[[-1, P]], channel_multiplier=1).then_inc(masks, 1)
            pool.dma_start(id_sb[0:1, NB:2 * NB], id1.rearrange("(o n) -> o n", o=1)).then_inc(id1_in, 16)

            def fill_bt(b, s):
                wait_from(pool, bxt_done, b - 1)
                nc.gpsimd.tensor_copy(bt_slot[:, s, :, :], bt[:, :, b, :].bitcast(F32)).then_inc(bt_filled, 1)

            pool.wait_ge(bt_ready, 1)
            fill_bt(0, 0)
            fill_bt(1, 1)
            pool.wait_ge(id1_in, 16)
            for b in range(NB):
                adapter = pool.value_load(id_sb[0:1, NB + b:NB + b + 1], min_val=0, max_val=NA1 - 1)
                pool.dma_start(rows[b * RK:(b + 1) * RK, :],
                               A1[bass.ds(adapter, 1)].rearrange("a r d -> (a r) d")).then_inc(a1rows_in, 16)
                pool.dma_start(b1_in[:, b, :], b1_v[bass.ds(adapter, 1)].rearrange("a p c -> p (a c)")
                               ).then_inc(b1_loaded, 16)
            with pool.Fori(1, NB // 2) as q:
                fill_bt(q * 2, 0)
                fill_bt(q * 2 + 1, 1)
            pool.wait_ge(amax_ready, 2)
            nc.gpsimd.partition_all_reduce(gmax[:, :], amax[:, :], P, bass.bass_isa.ReduceOp.max).then_inc(gmax_ready, 1)
            pool.wait_ge(raw_ready, 1)
            nc.gpsimd.tensor_tensor(a1_t[:, :, :, RK:2 * RK].rearrange("p b k r -> p k b r"),
                                    raw_a1.rearrange("p (k b r) -> p k b r", k=KC, b=NB),
                                    a1_t[:, :, :, 0:RK].bitcast(F32).rearrange("p b k r -> p k b r"),
                                    ALU.subtract).then_inc(lo_ready, 1)
            pool.wait_ge(raw_ready, 2)
            nc.gpsimd.tensor_tensor(b1_lo, raw_b1, b1_hi.bitcast(F32), ALU.subtract).then_inc(lo_ready, 1)

            def fill_slot(b, j):
                wait_from(pool, slot_used, b * 2 + (j - 1))
                nc.gpsimd.tensor_copy(u_slot[:, j, :], u_tok[:, b, j, :]).then_inc(slot_ready, 1)

            def fill_a1(b):
                wait_from(pool, h_done, b * 2)
                nc.gpsimd.tensor_copy(a1_b, a1_t[:, bass.ds(b, 1), :, :].bitcast(F32).rearrange("p o k r -> p k o r"
                                      ).to_broadcast([P, KC, 3, HR])).then_inc(a1b_ready, 1)

            pool.wait_ge(lo_ready, 1)
            pool.wait_ge(bxt_done, NB)
            fill_a1(0)
            with pool.Fori(0, KC) as i:
                pool.wait_ge(u_copied, i + 1)
                cols = bass.ds(i * P, P)
                nc.gpsimd.tensor_tensor(u_lo[:, cols], u_raw[:, cols], u_hi[:, cols].bitcast(F32),
                                        ALU.subtract).then_inc(u_split, 1)
            pool.wait_ge(u_ready, 1)
            fill_slot(0, 0)

            def step(t, b, j):
                go = Parts(t, b)
                if go.prev2:
                    pool.wait_ge(scaled_ready, t - 1)
                    pool.wait_ge(x1_copied, t - 1)
                    nc.gpsimd.tensor_tensor(out_slot[j], scaled, out_slot[j], ALU.add).then_inc(out_ready, 1)
                if not isinstance(t, int) or t + 2 < NT:
                    fill_slot(b + 1, j)
                    if j:
                        fill_a1(b + 1)

            def first_step():
                fill_slot(0, 1)
            first_step()
            step(0, 0, 0)
            step(1, 0, 1)
            with pool.Fori(1, NB - 1) as b:
                step(b * 2, b, 0)
                step(b * 2 + 1, b, 1)
            for t in range(NT - 2, NT + 2):
                step(t, t // 2, t % 2)

        @block.scalar
        def _(act):
            act.dma_start(id_sb[0:1, 0:NB], id0.rearrange("(o n) -> o n", o=1)).then_inc(id0_in, 16)
            act.dma_start(id_bc[:, :], id0.rearrange("(o n) -> o n", o=1).to_broadcast([P, NB])).then_inc(ids_in, 16)
            act.dma_start(w0_head, W0[0:NE, :]).then_inc(head_in, 16)
            with nc.allow_non_contiguous_dma(reason="small"):
                act.dma_start(m1[:, :, 0:RZ], Affn.rearrange("(p k) r -> p k r", p=P)).then_inc(affn_in, 16)
                act.dma_start(l_bc[:, :, :].rearrange("p e r -> p (e r)"),
                              Lm.rearrange("(o e) r -> o (e r)", o=1).to_broadcast([P, NE * RZ])).then_inc(bc_in, 16)
                act.dma_start(b0_bc[:, :], b0[0:NE].rearrange("(o e) -> o e", o=1).to_broadcast([P, NE])
                              ).then_inc(bc_in, 16)
                act.wait_ge(masks, 4)
                act.dma_start(expand[0:RZ, RZ + NE:NC], Lm.rearrange("e r -> r e")).then_inc(lt_in, 16)
            act.dma_start(split_in[0:RZ, :], Bmat[:, :]).then_inc(split_loaded, 16)
            act.dma_start(split_in[RZ:RZ + 1, :], b0.rearrange("(o n) -> o n", o=1)).then_inc(split_loaded, 16)
            act.dma_start(split_in[RZ + 1:RZ + 2, :], bb.rearrange("(o n) -> o n", o=1)).then_inc(split_loaded, 16)
            act.wait_ge(chain, 3)
            nc.scalar.copy(p_b[:, :, NC:NR], e16[0:2 * RK, :].unsqueeze(1).to_broadcast([2 * RK, NB, RK])
                           ).then_inc(p_through, 1)
            act.wait_ge(bt_done, 1)
            nc.scalar.copy(bt[:, :, :, 0:RK], pC[:, :].rearrange("p (k b r) -> p k b r", k=KC, b=NB)).then_inc(bt_high, 1)

            def prepass(q):
                for i in range(2):
                    b = q * 2 + i
                    for j in range(2):
                        act.wait_ge(xt_done, b * 2 + (j + 1))
                        wait_from(act, bxt_done, b - 1)
                        nc.scalar.copy(xt_hi[i][:, :, j * P:(j + 1) * P], pAB3[j]).then_inc(xt_high, 1)
                    act.wait_ge(wbt_done, b + 1)
                    nc.scalar.copy(wb_hi[:, :, bass.ds(b * P, P)], pC3).then_inc(wb_high, 1)
                    if not isinstance(b, int) or b >= 1:
                        copy_bx(b - 1, 1 - i)
                    if not isinstance(b, int) or b >= 2:
                        copy_z(b - 2)

            def copy_bx(b, i):
                act.wait_ge(bxt_done, b + 1)
                wait_from(act, z_done, b - 1)
                nc.scalar.copy(bx_t[:, i, :], pD[0:2 * RK, 0:2 * P]).then_inc(bxt_copied, 1)

            def copy_z(b):
                act.wait_ge(z_done, b + 1)
                nc.scalar.copy(z_sb[:, :, bass.ds(b, 1), :].rearrange("p j o c -> p j (o c)"),
                               pE[:, 0:2 * NR].rearrange("p (j c) -> p j c", j=2)).then_inc(z_copied, 1)

            prepass(0)
            with act.Fori(1, NB // 2) as q:
                prepass(q)
            copy_z(NB - 2)
            copy_bx(NB - 1, 1)

            def copy_w0t(q, s):
                act.wait_ge(w0t_done, q * 2 + (s + 1))
                wait_from(act, u_done, q * 2 + (s - 1))
                nc.scalar.copy(w0t_raw[s], pAB[s][:, :]).then_inc(w0t_copied, 1)

            def copy_u(q, s):
                act.wait_ge(u_done, q * 2 + (s + 1))
                cols = bass.ds(q * 2 * P + s * P, P)
                nc.scalar.copy(u_hi[:, cols], pDE[s][:, 0:P])
                nc.scalar.copy(u_raw[:, cols], pDE[s][:, 0:P]).then_inc(u_copied, 1)

            copy_w0t(0, 0)
            copy_z(NB - 1)
            copy_w0t(0, 1)
            copy_u(0, 0)
            act.wait_ge(b1_loaded, 16 * NB)
            nc.scalar.copy(b1_k.rearrange("p k (b r) -> p k b r", b=NB),
                           b1_in.rearrange("p b (k r) -> p k b r", k=KC)).then_inc(b1_ordered, 1)
            act.wait_ge(e1_in, 1)
            nc.scalar.activation(prob[:, :, :], logit[:, :, :], ACT.Exp).then_inc(e1_out, 1)
            act.wait_ge(a1t_done, 1)
            act.wait_ge(const_rows, 16 * 7)
            a1_src = pC[:, :].rearrange("p (k b r) -> p k b r", k=KC, b=NB)
            nc.scalar.copy(a1_t[:, :, :, 0:RK].rearrange("p b k r -> p k b r"), a1_src)
            nc.scalar.copy(raw_a1, pC[:, :]).then_inc(raw_ready, 1)
            copy_w0t(1, 0)
            copy_u(0, 1)
            act.wait_ge(e2_in, 1)
            nc.scalar.activation(gate[:, :, :], gate[:, :, :], ACT.Exp, scale=-2.0).then_inc(e2_out, 1)
            act.wait_ge(b1t_done, 1)
            nc.scalar.copy(b1_hi.rearrange("m (p k) -> m k p", k=KC), pC3)
            nc.scalar.copy(raw_b1.rearrange("m (p k) -> m k p", k=KC), pC3).then_inc(raw_ready, 1)
            copy_w0t(1, 1)
            with act.Fori(2, KC // 2) as q:
                copy_u(q - 1, 0)
                copy_w0t(q, 0)
                copy_u(q - 1, 1)
                copy_w0t(q, 1)
            copy_u(KC // 2 - 1, 0)
            copy_u(KC // 2 - 1, 1)

            def copy_w8(i):
                act.wait_ge(w8t_done, i + 1)
                nc.scalar.copy(w8_t[:, :, i * P:(i + 1) * P],
                               pABh[i % 4].rearrange("p (k c) -> p k c", k=KC)).then_inc(w8_act, 1)

            def step(t, b, j):
                go = Parts(t, b)
                if go.prev:
                    act.wait_ge(quant_ready, t)
                    wait_from(act, at_done, t - 1)
                    nc.scalar.activation(a_bf, quant, ACT.Copy, bias=-MAGIC).then_inc(abf_ready, 1)
                if go.next:
                    act.wait_ge(slot_used, t + 2)
                    wait_from(act, x1mm_done, t + 1)
                    nc.scalar.copy(ut[:, :], pE[0:U1, 0:P]).then_inc(ut_ready, 1)
                if isinstance(t, int) and t == -1:
                    for i in range(1, KC, 2):
                        copy_w8(i)
                if go.cur:
                    act.wait_ge(h_summed, t + 1)
                    wait_from(act, r_done, t)
                    nc.scalar.copy(ht[0:3 * HR, :], h_sum[:, :]).then_inc(h_rounded, 1)
                if go.prev:
                    act.wait_ge(at_done, t)
                    wait_from(act, acc_done, t - 1)
                    nc.scalar.copy(w8_bf[:, 1, :], pBh[0]).then_inc(at_ready, 1)
                if go.next:
                    act.wait_ge(x1t_done, t + 2)
                    nc.scalar.copy(x1t_hi, pC3).then_inc(hi_ready, 1)
                if go.cur:
                    wait_from(act, stored[j], b * 16)
                    nc.scalar.copy(out_slot[j], x1[:, j, :]).then_inc(x1_copied, 1)

            main_steps(act, step)

        @block.vector
        def _(dve):
            nc.vector.memset(ht[3 * HR:U2, :].bitcast(F32), 1.0).then_inc(ones_set, 1)
            links = [0]

            def link(instruction):
                links[0] += 1
                instruction.then_inc(chain, 1)
                dve.wait_ge(chain, links[0])

            dve.wait_ge(masks, 7)
            link(nc.vector.tensor_scalar(part[:, :], part[:, :], 4, None, ALU.logical_shift_right))
            link(nc.vector.tensor_copy(block_f[:, :], part[:, :]))
            link(nc.vector.tensor_reduce(e16[:, :], ident[:, :].rearrange("p (b r) -> p r b", b=NB), AX.X, ALU.add))
            dve.wait_ge(ids_in, 16)
            link(nc.vector.tensor_copy(id_f[:, :], id_bc[:, :]))
            link(nc.vector.tensor_scalar(onehot[:, :], id_f[:, :], block_f[:, :], None, ALU.is_equal))
            nc.vector.tensor_tensor(pick[:, :, :], onehot[:, :].unsqueeze(2).to_broadcast([P, NB, RK]),
                                    e16[:, :].unsqueeze(1).to_broadcast([P, NB, RK]), ALU.mult).then_inc(pick_ready, 1)
            dve.wait_ge(bt_high, 1)
            nc.vector.tensor_tensor(bt[:, :, :, RK:2 * RK], pC[:, :].rearrange("p (k b r) -> p k b r", k=KC, b=NB),
                                    bt[:, :, :, 0:RK].bitcast(F32), ALU.subtract).then_inc(bt_ready, 1)
            def split_x(b, i, j):
                dve.wait_ge(xt_high, b * 2 + (j + 1))
                nc.vector.tensor_tensor(xt_lo[i][:, :, j * P:(j + 1) * P], pAB3[j],
                                        xt_hi[i][:, :, j * P:(j + 1) * P].bitcast(F32), ALU.subtract).then_inc(xt_split, 1)

            def split_wb(b):
                dve.wait_ge(wb_high, b + 1)
                nc.vector.tensor_tensor(wb_lo[:, :, bass.ds(b * P, P)], pC3,
                                        wb_hi[:, :, bass.ds(b * P, P)].bitcast(F32), ALU.subtract).then_inc(wb_split, 1)

            split_x(0, 0, 0)
            split_x(0, 0, 1)
            split_wb(0)
            dve.wait_ge(p_step, 1)
            nc.vector.tensor_copy(m1[:, :, RZ:RZ + NE], pE[:, 0:KC * NE].rearrange("p (k e) -> p k e", k=KC)
                                  ).then_inc(p_copied, 1)
            split_x(1, 1, 0)
            dve.wait_ge(a0_loaded, 16 * NB)
            nc.vector.tensor_copy(a0_k.rearrange("p k (b r) -> p k b r", b=NB),
                                  a0_in.rearrange("p b (k r) -> p k b r", k=KC)).then_inc(a0_ordered, 1)
            split_x(1, 1, 1)
            split_wb(1)
            dve.wait_ge(p_step, 2)
            nc.vector.tensor_copy(p_t[:, :, :, :], pE[0:RZ + NE, 0:P].rearrange("m (b o r) -> m b o r", b=NB, o=1
                                  ).to_broadcast([RZ + NE, NB, 2, RK])).then_inc(p_copied, 1)
            dve.wait_ge(p_step, 3)
            nc.vector.tensor_copy(p_b[:, :, 0:NC], pE[0:2 * RK, 0:NB * NC].rearrange("p (b c) -> p b c", b=NB)
                                  ).then_inc(p_copied, 1)
            dve.wait_ge(split_loaded, 48)
            link(nc.vector.tensor_copy(split_hi, split_in))
            nc.vector.tensor_tensor(split_lo, split_in, split_hi.bitcast(F32), ALU.subtract).then_inc(split_done, 1)
            with dve.Fori(1, NB // 2) as q:
                for i in range(2):
                    split_x(q * 2 + i, i, 0)
                    split_x(q * 2 + i, i, 1)
                    split_wb(q * 2 + i)
            dve.wait_ge(z_copied, NB)
            dve.wait_ge(bc_in, 32)
            hs, ds_ = z_sb[:, 1, :, RZ:RZ + NE], z_sb[:, 1, :, RZ + NE:NC]
            link(nc.vector.tensor_tensor(hs, hs, b0_bc[:, :].unsqueeze(1).to_broadcast([P, NB, NE]), ALU.add))
            nc.vector.tensor_reduce(amax[:, 0:1], hs, AX.XY, ALU.max, apply_absolute_value=True).then_inc(amax_ready, 1)
            nc.vector.tensor_reduce(amax[:, 1:2], ds_, AX.XY, ALU.max, apply_absolute_value=True).then_inc(amax_ready, 1)
            dve.wait_ge(gmax_ready, 1)
            link(nc.vector.tensor_scalar(gmax[:, :], gmax[:, :], 1e-6, 2.0, ALU.max, ALU.mult))
            link(nc.vector.reciprocal(ginv[:, :], gmax[:, :]))
            link(nc.vector.tensor_scalar(logit[:, :, :], ds_, ginv[:, 1:2], None, ALU.mult))
            link(nc.vector.scalar_tensor_tensor(logit[:, :, :], hs, ginv[:, 0:1], logit[:, :, :], ALU.mult, ALU.add))
            link(nc.vector.tensor_reduce(stat[:, :], logit[:, :, :], AX.X, ALU.max))
            nc.vector.tensor_tensor(logit[:, :, :], logit[:, :, :], stat[:, :].unsqueeze(2).to_broadcast([P, NB, NE]),
                                    ALU.subtract).then_inc(e1_in, 1)
            dve.wait_ge(e1_out, 1)
            link(nc.vector.tensor_reduce(stat[:, :], prob[:, :, :], AX.X, ALU.add))
            link(nc.vector.reciprocal(stat[:, :], stat[:, :]))
            link(nc.vector.tensor_tensor(prob[:, :, :], prob[:, :, :],
                                         stat[:, :].unsqueeze(2).to_broadcast([P, NB, NE]), ALU.mult))
            for b in range(NB):
                last = nc.vector.max(top8[:, b, :], prob[:, b, :])
            link(last)
            nc.vector.tensor_tensor(gate[:, :, :], prob[:, :, :], top8[:, :, 1:2].to_broadcast([P, NB, NE]),
                                    ALU.subtract).then_inc(e2_in, 1)
            dve.wait_ge(e2_out, 1)
            link(nc.vector.tensor_scalar(gate[:, :, :], gate[:, :, :], 1.0, None, ALU.add))
            link(nc.vector.reciprocal(gate[:, :, :], gate[:, :, :]))
            link(nc.vector.tensor_tensor(gate[:, :, :], gate[:, :, :], prob[:, :, :], ALU.mult))
            link(nc.vector.tensor_reduce(stat[:, :], gate[:, :, :], AX.X, ALU.add))
            link(nc.vector.tensor_scalar(stat[:, :], stat[:, :], 1e-9, None, ALU.add))
            link(nc.vector.reciprocal(stat[:, :], stat[:, :]))
            link(nc.vector.tensor_tensor(gate[:, :, :], gate[:, :, :],
                                         stat[:, :].unsqueeze(2).to_broadcast([P, NB, NE]), ALU.mult))
            for b in range(NB):
                last = nc.vector.tensor_tensor(mixprod[:, b, :, :], gate[:, b, :].unsqueeze(1).to_broadcast([P, RZ, NE]),
                                               l_bc[:, :, :].rearrange("p e r -> p r e"), ALU.mult)
            link(last)
            link(nc.vector.tensor_reduce(pmix[:, :, :], mixprod[:, :, :, :], AX.X, ALU.add))
            nc.vector.memset(u_tok[:, :, :, 2 * NU:U1], 1.0).then_inc(ones_set, 1)
            for j in range(2):
                link(nc.vector.scalar_tensor_tensor(u_tok[:, :, j, RK:NU], z_sb[:, j, :, 0:RZ], 0.5, pmix[:, :, :],
                                                    ALU.mult, ALU.mult))
                link(nc.vector.tensor_copy(u_tok[:, :, j, 0:RK], z_sb[:, j, :, NC:NR]))
                link(nc.vector.tensor_copy(u_round[:, :, j, :], u_tok[:, :, j, 0:NU]))
                last = nc.vector.tensor_tensor(u_tok[:, :, j, NU:2 * NU], u_tok[:, :, j, 0:NU],
                                               u_round[:, :, j, :].bitcast(F32), ALU.subtract)
                if j == 0:
                    link(last)
            last.then_inc(u_ready, 1)
            dve.wait_ge(w8_in, 16)
            dve.wait_ge(b1_ordered, 1)
            dve.wait_ge(u_ready, 1)
            for i in range(KC):
                nc.vector.tensor_copy(w8_tile[i], w8_in8[:, i, :].bitcast(I8)).then_inc(w8_conv, 1)
            for i in range(0, KC, 2):
                dve.wait_ge(w8t_done, i + 1)
                nc.vector.tensor_copy(w8_t[:, :, i * P:(i + 1) * P],
                                      pABh[i % 4].rearrange("p (k c) -> p k c", k=KC)).then_inc(w8_dve, 1)

            def step(t, b, j):
                go = Parts(t, b)
                nj = 1 - j
                if go.cur:
                    dve.wait_ge(h_done, t + 1)
                    nc.vector.tensor_reduce(h_sum[:, :], pD[0:3 * HR, 0:2 * P].rearrange("m (c t) -> m t c", c=2),
                                            AX.X, ALU.add).then_inc(h_summed, 1)
                    dve.wait_ge(h_rounded, t + 1)
                    low = slice(2 * HR, 3 * HR)
                    nc.vector.tensor_tensor(ht[low, :], h_sum[low, :], ht[low, :].bitcast(F32),
                                            ALU.subtract).then_inc(ht_ready, 1)
                if go.prev2:
                    dve.wait_ge(acc_done, t - 1)
                    wait_from(dve, out_ready, t - 2)
                    nc.vector.scalar_tensor_tensor(scaled, pB[:, :], a_scale[:, j:j + 1], ws_bc,
                                                   ALU.mult, ALU.mult).then_inc(scaled_ready, 1)
                if go.next:
                    dve.wait_ge(x1mm_done, t + 2)
                    dve.wait_ge(xm_in[nj], (b + (1 if j else 0)) * 16 + 16)
                    wait_from(dve, x1_copied, t)
                    nc.vector.tensor_tensor(x1[:, nj, :], pC[:, :], x_ring[:, nj, :], ALU.add).then_inc(x1_ready, 1)
                if go.cur:
                    dve.wait_ge(r0_done, t + 1)
                    nc.vector.tensor_reduce(mag2[:, 0:1], pA[:, 0:HALF], AX.X, ALU.max, apply_absolute_value=True
                                            ).then_inc(mag_ready, 1)
                    dve.wait_ge(r_done, t + 1)
                    nc.vector.tensor_reduce(mag2[:, 1:2], pA[:, HALF:D], AX.X, ALU.max, apply_absolute_value=True
                                            ).then_inc(mag_ready, 1)
                    dve.wait_ge(mag_ready, t * 2 + 2)
                    nc.vector.tensor_tensor(mag[:, :], mag2[:, 0:1], mag2[:, 1:2], ALU.max).then_inc(mag1_ready, 1)
                    dve.wait_ge(mag1_ready, t + 1)
                    nc.vector.tensor_scalar(a_scale[:, j:j + 1], mag[:, :], 1.0 / QMAX, TINY, ALU.mult, ALU.max
                                            ).then_inc(scale_ready, 1)
                    dve.wait_ge(scale_ready, t + 1)
                    nc.vector.reciprocal(a_inv[:, :], a_scale[:, j:j + 1]).then_inc(inv_ready, 1)
                    dve.wait_ge(inv_ready, t + 1)
                    wait_from(dve, abf_ready, t)
                    nc.vector.tensor_scalar(quant, pA[:, :], a_inv[:, :], MAGIC, ALU.mult, ALU.add
                                            ).then_inc(quant_ready, 1)
                if go.next:
                    dve.wait_ge(hi_ready, t + 2)
                    nc.vector.tensor_tensor(x1t_lo, pC3, x1t_hi.bitcast(F32),
                                            ALU.subtract).then_inc(x1lo_ready, 1)

            dve.wait_ge(w0t_done, KC)
            dve.wait_ge(ws_in, 16)
            main_steps(dve, step)

        @block.tensor
        def _(pe):
            pe.wait_ge(masks, 7)
            pe.wait_ge(b_in, 16)
            pe.wait_ge(pick_ready, 1)
            pick_m = pick[:, :, :].rearrange("p b r -> p (b r)")
            for k in range(KC):
                last = nc.tensor.matmul(pC3[:, k, :], rows[:, k * P:(k + 1) * P], pick_m, start=True, stop=True)
            last.then_inc(bt_done, 1)

            def transpose_x(b, i, j):
                s = 2 * i + j
                pe.wait_ge(x_in[s], (b - i) * 8 + 16)
                wait_from(pe, xt_split, b * 2 + (j - 1))
                for k in range(KC):
                    last = nc.tensor.transpose(pAB3[j][:, k, :], x_ring[:, s, k * P:(k + 1) * P], ident[:, :])
                last.then_inc(xt_done, 1)

            def transpose_wb(b, i):
                pe.wait_ge(wb_in[i], (b - i) * 8 + 16)
                wait_from(pe, wb_split, b)
                for k in range(KC):
                    last = nc.tensor.transpose(pC3[:, k, :], wb_ring[:, i, k * P:(k + 1) * P], ident[:, :])
                last.then_inc(wbt_done, 1)

            def project(b, i):
                pe.wait_ge(bt_filled, b + 1)
                pe.wait_ge(xt_split, b * 2 + 2)
                wait_from(pe, bxt_copied, b)
                for k in range(KC):
                    nc.tensor.matmul(pD[0:2 * RK, 0:2 * P], bt_slot[:, i, k, :], xt_hi[i][:, k, :],
                                     start=(k == 0), stop=False)
                    last = nc.tensor.matmul(pD[0:RK, 0:2 * P], bt_slot[:, i, k, 0:RK], xt_lo[i][:, k, :],
                                            start=False, stop=(k == KC - 1))
                last.then_inc(bxt_done, 1)

            def route(b, i):
                pe.wait_ge(bxt_copied, b + 1)
                wait_from(pe, z_copied, b)
                for j in range(2):
                    last = nc.tensor.matmul(pE[:, j * NR:(j + 1) * NR], bx_t[:, i, j * P:(j + 1) * P],
                                            p_b[:, bass.ds(b, 1), :].rearrange("p o c -> p (o c)"),
                                            start=True, stop=True)
                last.then_inc(z_done, 1)

            def prepass(q):
                for i in range(2):
                    b = q * 2 + i
                    transpose_x(b, i, 0)
                    if not isinstance(b, int) or b >= 2:
                        route(b - 2, i)
                    transpose_x(b, i, 1)
                    if isinstance(b, int) and b == 0:
                        pe.wait_ge(bt_ready, 1)
                    transpose_wb(b, i)
                    if isinstance(b, int) and b == 0:
                        head_of_w0()
                    if isinstance(b, int) and b == 1:
                        head_by_a()
                    if not isinstance(b, int) or b >= 1:
                        project(b - 1, 1 - i)
                    if isinstance(b, int) and b == 1:
                        to_p_b()

            def head_of_w0():
                pe.wait_ge(head_in, 16)
                for k in range(KC):
                    last = nc.tensor.transpose(pE[:, k * NE:(k + 1) * NE], w0_head[:, k:D:KC], ident[0:NE, 0:NE])
                last.then_inc(p_step, 1)

            def head_by_a():
                pe.wait_ge(p_copied, 1)
                pe.wait_ge(affn_in, 16)
                pe.wait_ge(a0_ordered, 1)
                for k in range(KC):
                    last = nc.tensor.matmul(pE[0:RZ + NE, 0:P], m1[:, k, :], a0_k[:, k, :], start=(k == 0), stop=(k == KC - 1))
                last.then_inc(p_step, 1)

            def to_p_b():
                pe.wait_ge(p_copied, 2)
                pe.wait_ge(lt_in, 16)
                for b in range(NB):
                    last = nc.tensor.matmul(pE[0:2 * RK, b * NC:(b + 1) * NC],
                                            p_t[:, b, :, :].rearrange("m h r -> m (h r)"), expand[:, :],
                                            start=True, stop=True)
                last.then_inc(p_step, 1)

            prepass(0)
            pe.wait_ge(p_copied, 3)
            pe.wait_ge(p_through, 1)
            with pe.Fori(1, NB // 2) as q:
                prepass(q)

            def transpose_w0(q, s):
                pe.wait_ge(w0_in[s], q * 16 + 16)
                wait_from(pe, w0t_copied, q * 2 + (s - 1))
                for k in range(KC):
                    last = nc.tensor.transpose(pAB3[s][:, k, :], w0_ring[:, s, k:D:KC], ident[:, :])
                last.then_inc(w0t_done, 1)

            def apply_w0(q, s):
                pe.wait_ge(w0t_copied, q * 2 + (s + 1))
                wait_from(pe, u_copied, q * 2 + (s - 1))
                for k in range(KC):
                    last = nc.tensor.matmul(pDE[s][:, 0:P], a0_k[:, k, :], w0t_raw[s][:, k * P:(k + 1) * P],
                                            start=(k == 0), stop=(k == KC - 1))
                last.then_inc(u_done, 1)

            route(NB - 2, 0)
            project(NB - 1, 1)
            pe.wait_ge(xt_split, NT)
            transpose_w0(0, 0)
            route(NB - 1, 1)
            transpose_w0(0, 1)
            pe.wait_ge(bxt_copied, NB)
            apply_w0(0, 0)
            pe.wait_ge(a1rows_in, 16 * NB)
            pe.wait_ge(wb_split, KC)
            for k in range(KC):
                last = nc.tensor.transpose(pC3[:, k, :], rows[:, k * P:(k + 1) * P], ident[:, :])
            last.then_inc(a1t_done, 1)
            transpose_w0(1, 0)
            pe.wait_ge(z_copied, NB)
            apply_w0(0, 1)
            pe.wait_ge(b1_ordered, 1)
            pe.wait_ge(raw_ready, 1)
            for k in range(KC):
                last = nc.tensor.transpose(pC3[:, k, :], b1_k[:, k, :], ident[:, :])
            last.then_inc(b1t_done, 1)
            transpose_w0(1, 1)
            with pe.Fori(2, KC // 2) as q:
                apply_w0(q - 1, 0)
                transpose_w0(q, 0)
                apply_w0(q - 1, 1)
                transpose_w0(q, 1)
            apply_w0(KC // 2 - 1, 0)
            apply_w0(KC // 2 - 1, 1)

            def transpose_w8(i):
                pe.wait_ge(w8_conv, i + 1)
                wait_from(pe, (w8_dve, w8_act)[i % 2], (i - 2) // 2)
                for k in range(KC):
                    last = nc.tensor.transpose(pABh[i % 4][:, k * P:(k + 1) * P], w8_tile[i][:, k * P:(k + 1) * P],
                                               ident_bf[:, :])
                last.then_inc(w8t_done, 1)

            def step(t, b, j):
                go = Parts(t, b)
                nb = b + (1 if j else 0)
                if go.next:
                    pe.wait_ge(slot_ready, t + 2)
                    wait_from(pe, ut_ready, t + 1)
                    nc.tensor.transpose(pE[0:U1, 0:P], u_slot[:, 1 - j, :], ident[:, :]).then_inc(slot_used, 1)
                if isinstance(t, int) and t == -1:
                    for i in range(KC):
                        transpose_w8(i)
                if isinstance(t, int) and t == 0:
                    pe.wait_ge(w8_dve, KC // 2)
                    pe.wait_ge(w8_act, KC // 2)
                if go.cur:
                    pe.wait_ge(hi_ready, t + 1)
                    pe.wait_ge(x1lo_ready, t + 1)
                    pe.wait_ge(a1b_ready, b + 1)
                    wait_from(pe, h_summed, t)
                    for k in range(KC):
                        last = nc.tensor.matmul(pD[0:3 * HR, 0:2 * P], a1_b[:, k, :, :].rearrange("p c r -> p (c r)"),
                                                x1t_both[:, k, :], start=(k == 0), stop=(k == KC - 1))
                    last.then_inc(h_done, 1)
                    wait_from(pe, quant_ready, t)

                def product(half):
                    cols = slice(half * HALF, (half + 1) * HALF)
                    for k in range(KC):
                        nc.tensor.matmul(pA[:, cols], x1t_hi[:, k, :], wb_hi[:, k, cols], start=(k == 0), stop=False)
                        nc.tensor.matmul(pA[:, cols], x1t_hi[:, k, :], wb_lo[:, k, cols], start=False, stop=False)
                        nc.tensor.matmul(pA[:, cols], x1t_lo[:, k, :], wb_hi[:, k, cols], start=False, stop=False)

                def lora(half):
                    cols = slice(half * HALF, (half + 1) * HALF)
                    return nc.tensor.matmul(pA[:, cols], ht[:, :], lora_r[:, cols], start=False, stop=True)

                if go.cur:
                    product(0)
                if go.next:
                    pe.wait_ge(ut_ready, t + 2)
                    pe.wait_ge(upd_in, nb * 48 + 48)
                    wait_from(pe, x1lo_ready, t + 1)
                    for half in range(2):
                        cols = slice(half * HALF, (half + 1) * HALF)
                        nc.tensor.matmul(pC[:, cols], ut[:, :], upd_hi[:, cols], start=True, stop=False)
                        last = nc.tensor.matmul(pC[:, cols], ut[0:NU, :], upd_lo[:, cols], start=False, stop=True)
                    last.then_inc(x1mm_done, 1)
                if go.prev:
                    pe.wait_ge(abf_ready, t)
                    wait_from(pe, scaled_ready, t - 1)
                    for k in range(KC):
                        last = nc.tensor.transpose(pBh[0][:, k * P:(k + 1) * P], a_bf[:, k * P:(k + 1) * P], ident_bf[:, :])
                    last.then_inc(at_done, 1)
                if go.cur:
                    pe.wait_ge(ht_ready, t + 1)
                    pe.wait_ge(lora_in, (b + 1) * 16 * 6)
                    lora(0).then_inc(r0_done, 1)
                    product(1)
                    lora(1).then_inc(r_done, 1)
                if go.next:
                    pe.wait_ge(x1_ready, t + 2)
                    for k in range(KC):
                        last = nc.tensor.transpose(pC3[:, k, :], x1[:, 1 - j, k * P:(k + 1) * P], ident[:, :])
                    last.then_inc(x1t_done, 1)
                if go.prev:
                    pe.wait_ge(at_ready, t)
                    for half in range(2):
                        cols = slice(half * HALF, (half + 1) * HALF)
                        for k in range(KC):
                            last = nc.tensor.matmul(pB[:, cols], a_t[:, k, :], w8_t[:, k, cols],
                                                    start=(k == 0), stop=(k == KC - 1))
                    last.then_inc(acc_done, 1)

            pe.wait_ge(ones_set, 2)
            pe.wait_ge(const_rows, 16 * 7)
            main_steps(pe, step)


_INS = ['x', 'itok_B_3_7', 'itok_B_6_15', 'L0_cond_A', 'L0_cond_B', 'L0_ffn_W', 'L0_ffn_b', 'L0_ffn_A', 'L0_ffn_Bmat',
        'L0_ffn_LiMEs', 'L1_cond_base_weight', 'L1_cond_base_bias', 'L1_cond_lora_A_w', 'L1_cond_lora_B_w',
        'L1_ffn_weight', 'L1_ffn_weight_scale']


def kernel(**inputs):
    import numpy as _np
    import concourse.bacc as _bacc
    from concourse import mybir as _mybir
    from concourse.bass_utils import run_bass_kernel_spmd as _run

    nc = _bacc.Bacc("TRN2", target_bir_lowering=False, num_devices=1)
    arrays, args = {}, []
    for name in _INS:
        a = _np.ascontiguousarray(inputs[name])
        if a.dtype.itemsize == 1:
            a = a.view(_np.int32)
        arrays[f"in_{name}_dram"] = a
        args.append(nc.dram_tensor(f"in_{name}_dram", a.shape, _mybir.dt.from_np(a.dtype), kind="ExternalInput").ap())
    args.append(nc.dram_tensor("out_0_dram", (NB, 2 * P, D), F32, kind="ExternalOutput").ap())
    ffn_kernel(nc, *args)
    r = _run(nc, [arrays], core_ids=[0])
    return r.results[0]["out_0_dram"]
```

```python
import concourse.bass as bass
from concourse import mybir
from contextlib import ExitStack

F32 = mybir.dt.float32
F32R = mybir.dt.float32r
BF16 = mybir.dt.bfloat16
I8 = mybir.dt.int8
I32 = mybir.dt.int32
ALU = mybir.AluOpType
ACT = mybir.ActivationFunctionType
AX = mybir.AxisListType

P = 128
NB = 8
D = 1024
KC = D // P
HALF = D // 2
HALVES = (slice(0, HALF), slice(HALF, D))
ENDING = (HALVES[0], slice(HALF, HALF + HALF // 2), slice(HALF + HALF // 2, D))
HALF_CHUNKS = (range(0, KC // 2), range(KC // 2, KC))
RK = 16
NA0, NA1 = 8, 32
RZ = 32
NE = 8
NT = 2 * NB
NU = RK + RZ
NC = RZ + 2 * NE
NR = NC + RK
U1 = 2 * NU + 2
HR = 2 * RK
U2 = 3 * HR + 2
WARM_UP = 16
MAGIC = 1.5 * 2.0 ** 23
QMAX = 127.0
TINY = 2.0 ** -126


def ffn_kernel(nc, x, id0, id1, A0, B0, W0, b0, Affn, Bmat, Lm, Wb, bb, A1, B1, W8, ws, out):
    ctx = ExitStack()
    with ctx:
        def sb(name, shape, dt=F32):
            return ctx.enter_context(nc.sbuf_tensor(name, shape, dt))

        def sem(name):
            return ctx.enter_context(nc.semaphore(name))

        wb_hi = sb("wb_hi", [P, KC, D], F32R)
        wb_lo = sb("wb_lo", [P, KC, D], F32R)
        w8_t = sb("w8_t", [P, KC, D], BF16)
        x_ring = sb("x_ring", [P, 4, D])
        w0_ring = sb("w0_ring", [P, 2, D])
        wb_ring = sb("wb_ring", [P, 2, D])
        w8_bf = sb("w8_bf", [P, 2, D], BF16)
        arena = sb("arena", [P, 4, D])
        bt = sb("bt", [P, KC, NB, 2 * RK], F32R)
        slots = sb("slots", [P, 3 * KC * HR], F32R)
        bt_slot = slots[:, 0:2 * KC * HR].rearrange("p (s k r) -> p s k r", s=2, k=KC)
        a1_b = slots[:, :].rearrange("p (k c r) -> p k c r", k=KC, c=3)
        a1_t = sb("a1_t", [P, NB, KC, 2 * RK], F32R)
        ub = sb("ub", [P, 4, D], F32R)
        u_hi, u_lo = ub[:, 0, :], ub[:, 1, :]
        b1_hi, b1_lo = ub[:, 2, :], ub[:, 3, :]
        right = sb("right", [P, 3, D], F32R)
        upd_hi, upd_lo, lora_r = right[0:U1, 0, :], right[0:NU, 1, :], right[0:U2, 2, :]
        x1t = sb("x1t", [P, 2, D], F32R)
        x1t_both = x1t[:, :, :].rearrange("p s d -> p (s d)").rearrange("p (k c) -> p k c", k=KC)
        x1t_hi, x1t_lo = x1t_both[:, :, 0:P], x1t_both[:, :, P:2 * P]
        xt_hi = [v.rearrange("p s d -> p (s d)").rearrange("p (k c) -> p k c", k=KC)
                 for v in (x1t[:, :, :], ub[:, 0:2, :])]
        xt_lo = [v.rearrange("p s d -> p (s d)").rearrange("p (k c) -> p k c", k=KC)
                 for v in (right[:, 0:2, :], ub[:, 2:4, :])]
        ut = sb("ut", [U1, P], F32R)
        ht = sb("ht", [U2, P], F32R)
        h_sum = sb("h_sum", [3 * HR, P])
        ident = sb("ident", [P, P])
        ident_bf = sb("ident_bf", [P, P], BF16)
        id_sb = sb("id_sb", [1, NB], I32)
        id_bc = sb("id_bc", [P, NB], I32)
        id_f = sb("id_f", [P, NB])
        part = sb("part", [P, 1], I32)
        block_f = sb("block_f", [P, 1])
        onehot = sb("onehot", [P, NB])
        e16 = sb("e16", [P, RK])
        pick = sb("pick", [P, NB, RK])
        expand = sb("expand", [RZ + NE, NC])
        p_t = sb("p_t", [RZ + NE, NB, 2, RK])
        p_b = sb("p_b", [2 * RK, NB, NR])
        bx_t = sb("bx_t", [2 * RK, 2, 2 * P])
        z_sb = sb("z_sb", [P, 2, NB, NR])
        l_bc = sb("l_bc", [P, NE, RZ])
        b0_bc = sb("b0_bc", [P, NE])
        amax = sb("amax", [P, 2])
        gmax = sb("gmax", [P, 2])
        ginv = sb("ginv", [P, 2])
        logit = sb("logit", [P, NB, NE])
        prob = sb("prob", [P, NB, NE])
        gate = sb("gate", [P, NB, NE])
        top8 = sb("top8", [P, NB, NE])
        stat = sb("stat", [P, NB])
        pmix = sb("pmix", [P, NB, RZ])
        u_slot = sb("u_slot", [P, 2, U1])
        mag2 = sb("mag2", [P, 2])
        mag = sb("mag", [P, 1])
        a_scale = sb("a_scale", [P, 2])
        a_inv = sb("a_inv", [P, 1])

        early = w8_t[:, :, :].rearrange("p k c -> p (k c)").bitcast(F32)
        a0_k = early[:, 0:D].rearrange("p (k c) -> p k c", k=KC)
        b1_k = early[:, D:2 * D].rearrange("p (k c) -> p k c", k=KC)
        rows = early[:, 2 * D:3 * D]
        m1 = early[:, 3 * D:3 * D + KC * (RZ + NE)].rearrange("p (k c) -> p k c", k=KC)
        split_in = arena[0:RZ + 2, 0, :]
        w0_head = arena[0:NE, 1, :]
        raw_a1, raw_b1 = arena[:, 0, :], x_ring[:, 0, :]
        ws_bc = arena[:, 0, :]
        u_raw = arena[:, 1, :]
        a0_in = arena[:, 2, :].rearrange("p (b c) -> p b c", b=NB)
        w0t_raw = [arena[:, 2 + s, :] for s in range(2)]
        b1_in = w8_bf[:, :, :].rearrange("p s d -> p (s d)").bitcast(F32).rearrange("p (b c) -> p b c", b=NB)
        split_out = a1_t[0:RZ + 2, :, :, :].rearrange("p b k c -> p (b k c)")
        split_hi, split_lo = split_out[:, 0:D], split_out[:, D:2 * D]
        w8_in8 = wb_ring[:, :, :].rearrange("p s d -> p (s d)").bitcast(I32).rearrange("p (k c) -> p k c", k=KC)
        w8_tile = [v.bitcast(BF16)[:, h * D:(h + 1) * D] if v is not None else w8_bf[:, h, :]
                   for v in (None, x_ring[:, 1, :], x_ring[:, 2, :], x_ring[:, 3, :]) for h in range(2)]
        mixprod = x_ring[:, 2:4, :].rearrange("p s (b r e) -> p (s b) r e", r=RZ, e=NE)
        u_round = x_ring[:, 2, 0:NT * NU].rearrange("p (b j c) -> p b j c", b=NB, j=2).bitcast(F32R)
        u_tok = bt[:, :, :, :].rearrange("p k b r -> p (k b r)")[:, 0:NT * U1].bitcast(F32).rearrange(
            "p (b j c) -> p b j c", b=NB, j=2)
        a_bf = w8_bf[:, 0, :]
        a_t = w8_bf[:, 1, :].rearrange("p (k c) -> p k c", k=KC)
        out_slot = [x_ring[:, 2 + s, :] for s in range(2)]
        x1 = w0_ring
        quant = wb_ring[:, 0, :]
        scaled = wb_ring[:, 1, :]

        def pb(name, shape, dt=F32):
            return ctx.enter_context(nc.psum_tensor(name, shape, dt))

        pA = pb("pA", [P, D])
        pB = pb("pB", [P, D])
        pC = pb("pC", [P, D])
        pD = pb("pD", [P, HALF])
        pE = pb("pE", [P, HALF])
        pA3, pB3, pC3 = (v[:, :].rearrange("p (k c) -> p k c", k=KC) for v in (pA, pB, pC))
        pABh = [v[:, s * HALF:(s + 1) * HALF].bitcast(BF16) for v in (pA, pB) for s in range(2)]
        pBh, pCh = pABh[2:], [pC[:, s * HALF:(s + 1) * HALF].bitcast(BF16) for s in range(2)]
        ending = [pB[:, 0:HALF], pB[:, HALF:HALF + HALF // 2], pC[:, 0:HALF // 2]]
        pDE = [pD, pE]
        pAB = [pA, pB]
        pAB3 = [pA3, pB3]

        b_in, ids_in, head_in, affn_in = sem("b_in"), sem("ids_in"), sem("head_in"), sem("affn_in")
        a0_first, a0_second = sem("a0_first"), sem("a0_second")
        split_loaded, lt_in, bc_in = sem("split_loaded"), sem("lt_in"), sem("bc_in")
        id1_in, a1rows_in, b1_loaded = sem("id1_in"), sem("a1rows_in"), sem("b1_loaded")
        masks = sem("masks")
        ones_set = sem("ones_set")
        x_in = [sem(f"x_in{s}") for s in range(4)]
        wb_in = [sem(f"wb_in{s}") for s in range(2)]
        w0_in = [sem(f"w0_in{s}") for s in range(2)]
        w8_in = sem("w8_in")
        chain = sem("chain")
        pick_ready = sem("pick_ready")
        bt_done, bt_high, bt_ready, bt_filled = sem("bt_done"), sem("bt_high"), sem("bt_ready"), sem("bt_filled")
        a0_ordered, b1_ordered = sem("a0_ordered"), sem("b1_ordered")
        p_through = sem("p_through")
        p_step, p_copied = sem("p_step"), sem("p_copied")
        split_done = sem("split_done")
        xt_done, xt_high, xt_split = sem("xt_done"), sem("xt_high"), sem("xt_split")
        wbt_done, wb_high, wb_split = sem("wbt_done"), sem("wb_high"), sem("wb_split")
        bxt_done, bxt_copied = sem("bxt_done"), sem("bxt_copied")
        z_done, z_copied = sem("z_done"), sem("z_copied")
        a1t_done, b1t_done = sem("a1t_done"), sem("b1t_done")
        raw_ready, lo_ready = sem("raw_ready"), sem("lo_ready")
        w0t_done, w0t_copied = sem("w0t_done"), sem("w0t_copied")
        u_done, u_copied = sem("u_done"), sem("u_copied")
        u_split = sem("u_split")
        w8_conv, w8t_done = sem("w8_conv"), sem("w8t_done")
        w8_dve, w8_act = sem("w8_dve"), sem("w8_act")
        const_rows = sem("const_rows")
        ws_in = sem("ws_in")
        amax_ready, gmax_ready = sem("amax_ready"), sem("gmax_ready")
        e1_in, e1_out, e2_in, e2_out = sem("e1_in"), sem("e1_out"), sem("e2_in"), sem("e2_out")
        u_ready = sem("u_ready")
        xm_in = [sem(f"xm_in{s}") for s in range(2)]
        upd_first = sem("upd_first")
        upd_in, lora_in, a1b_ready = sem("upd_in"), sem("lora_in"), sem("a1b_ready")
        slot_ready, slot_used = sem("slot_ready"), sem("slot_used")
        ut_ready = sem("ut_ready")
        x1mm_done, x1_ready, x1_copied = sem("x1mm_done"), sem("x1_ready"), sem("x1_copied")
        x1t_done, hi_ready, x1lo_ready = sem("x1t_done"), sem("hi_ready"), sem("x1lo_ready")
        h_done, h_summed, h_rounded, ht_ready = sem("h_done"), sem("h_summed"), sem("h_rounded"), sem("ht_ready")
        r0_done, r_done = sem("r0_done"), sem("r_done")
        mag_ready, mag1_ready = sem("mag_ready"), sem("mag1_ready")
        scale_ready, inv_ready = sem("scale_ready"), sem("inv_ready")
        quant_ready, abf_ready = sem("quant_ready"), sem("abf_ready")
        at_done, at_ready = sem("at_done"), sem("at_ready")
        acc_done, scaled_ready, out_ready = sem("acc_done"), sem("scaled_ready"), sem("out_ready")
        stored = [sem(f"stored{s}") for s in range(2)]

        x_t = x.rearrange("b (p j) d -> b j p d", j=2)
        out_t = out.rearrange("b (p j) d -> b j p d", j=2)
        a0_v = A0.rearrange("a (p k) r -> a p (k r)", p=P)
        b1_v = B1.rearrange("a (p k) r -> a p (k r)", p=P)

        def wait_from(engine, semaphore, count):
            if not isinstance(count, int) or count > 0:
                engine.wait_ge(semaphore, count)

        class Parts:
            def __init__(self, t):
                self.ends = isinstance(t, int) and t == NT
                self.a_t_bank = pCh if self.ends else pBh
                self.cur = not isinstance(t, int) or 0 <= t < NT
                self.prev = not isinstance(t, int) or 0 <= t - 1 < NT
                self.prev2 = not isinstance(t, int) or 0 <= t - 2 < NT
                self.next = not isinstance(t, int) or 0 <= t + 1 < NT

        def main_steps(engine, step):
            step(0, 0, 0)
            step(1, 0, 1)
            with engine.Fori(1, NB - 1) as b:
                step(b * 2, b, 0)
                step(b * 2 + 1, b, 1)
            step(NT - 2, NB - 1, 0)
            step(NT - 1, NB - 1, 1)
            step(NT, NB, 0)
            step(NT + 1, NB, 1)

        def gather_a0(engine, batches, loaded):
            engine.wait_ge(ids_in, 16)
            for b in batches:
                adapter = engine.value_load(id_bc[0:1, b:b + 1], min_val=0, max_val=NA0 - 1)
                engine.dma_start(a0_in[:, b, :], a0_v[bass.ds(adapter, 1)].rearrange("a p c -> p (a c)")
                                 ).then_inc(loaded, 16)

        block = ctx.enter_context(nc.Block())

        @block.sync
        def _(sp):
            def move(dst, src):
                return sp.dma_start(dst.bitcast(F32), src.bitcast(F32))

            sp.dma_start(rows, B0.rearrange("a r d -> (a r) d")).then_inc(b_in, 16)

            def load_prepass(q):
                for s in range(4):
                    wait_from(sp, xt_done, q * 4 + (s - 3))
                    sp.dma_start(x_ring[:, s, :], x_t[q * 2 + s // 2, s % 2]).then_inc(x_in[s], 16)
                    if s % 2:
                        wait_from(sp, wbt_done, q * 2 + (s // 2 - 1))
                        sp.dma_start(wb_ring[:, s // 2, :], Wb[bass.ds(q * 2 * P + s // 2 * P, P), :]
                                     ).then_inc(wb_in[s // 2], 16)

            load_prepass(0)
            gather_a0(sp, range(0, NB // 2), a0_first)
            with sp.Fori(1, NT // 4) as q:
                load_prepass(q)

            def load_w0(q, s):
                wait_from(sp, w0t_done, q * 2 + (s - 1))
                sp.dma_start(w0_ring[:, s, :], W0[bass.ds(q * 2 * P + s * P, P), :]).then_inc(w0_in[s], 16)

            load_w0(0, 0)
            load_w0(0, 1)
            sp.wait_ge(wbt_done, KC)
            sp.dma_start(w8_in8, W8.rearrange("(k p) c -> p k c", p=P)).then_inc(w8_in, 16)
            load_w0(1, 0)
            sp.wait_ge(split_done, 1)
            sp.wait_ge(bxt_done, NB - 1)
            for row, src in ((2 * NU, split_hi[RZ:RZ + 1]), (2 * NU + 1, split_lo[RZ:RZ + 1])):
                move(upd_hi[row:row + 1, :], src).then_inc(const_rows, 16)
            for row, src in ((3 * HR, split_hi[RZ + 1:RZ + 2]), (3 * HR + 1, split_lo[RZ + 1:RZ + 2])):
                move(lora_r[row:row + 1, :], src).then_inc(const_rows, 16)
            move(upd_hi[RK:NU, :], split_hi[0:RZ]).then_inc(const_rows, 16)
            move(upd_hi[NU + RK:2 * NU, :], split_hi[0:RZ]).then_inc(const_rows, 16)
            move(upd_lo[RK:NU, :], split_lo[0:RZ]).then_inc(const_rows, 16)
            load_w0(1, 1)
            with sp.Fori(2, KC // 2) as q:
                load_w0(q, 0)
                load_w0(q, 1)

            def load_x(b, j):
                wait_from(sp, x1_ready, (b * 2 + (j - 1)) * 2)
                sp.dma_start(x_ring[:, j, :], x_t[b, j]).then_inc(xm_in[j], 16)

            def load_update(b):
                wait_from(sp, x1mm_done, b * 4)
                move_update(b, slice(0, D), 0, upd_in)

            def move_update(b, cols, made, there):
                wait_from(sp, u_copied, made)
                move(upd_hi[0:RK, cols], u_hi[b * RK:(b + 1) * RK, cols]).then_inc(there, 16)
                move(upd_hi[NU:NU + RK, cols], u_hi[b * RK:(b + 1) * RK, cols]).then_inc(there, 16)
                wait_from(sp, u_split, made)
                move(upd_lo[0:RK, cols], u_lo[b * RK:(b + 1) * RK, cols]).then_inc(there, 16)

            def load_lora(b):
                wait_from(sp, r_done, b * 2)
                for i, part_of_b1 in enumerate((b1_hi, b1_hi, b1_lo, b1_lo, b1_hi, b1_hi)):
                    move(lora_r[i * RK:(i + 1) * RK, :], part_of_b1[b * RK:(b + 1) * RK, :]).then_inc(lora_in, 16)

            def store(b, j):
                sp.wait_ge(out_ready, (b * 2 + (j + 1)) * 2)
                sp.dma_start(out_t[b, j], out_slot[j]).then_inc(stored[j], 16)

            sp.wait_ge(lo_ready, 2)
            sp.dma_start(ws_bc, ws.rearrange("n o -> o n").to_broadcast([P, D])).then_inc(ws_in, 16)
            load_x(0, 0)
            move_update(0, HALVES[0], KC // 2, upd_first)
            load_lora(0)
            move_update(0, HALVES[1], KC, upd_in)
            sp.wait_ge(w8t_done, 4)
            load_x(0, 1)
            load_x(1, 0)
            load_update(1)
            load_x(1, 1)
            load_lora(1)
            for b in range(1, NB - 1):
                load_x(b + 1, 0)
                store(b - 1, 0)
                load_update(b + 1)
                load_x(b + 1, 1)
                store(b - 1, 1)
                load_lora(b + 1)
            store(NB - 2, 0)
            store(NB - 2, 1)
            store(NB - 1, 0)
            for i, cols in enumerate(ENDING):
                sp.wait_ge(out_ready, (NT - 1) * 2 + 1 + i)
                sp.dma_start(out_t[NB - 1, 1][:, cols], out_slot[1][:, cols]).then_inc(stored[1], 16)
            sp.wait_ge(stored[0], 16 * NB)
            sp.wait_ge(stored[1], 16 * (NB - 1 + len(ENDING)))

        @block.gpsimd
        def _(pool):
            nc.gpsimd.memset(ident[:, :], 0.0).then_inc(masks, 1)
            nc.gpsimd.iota(part[:, :], pattern=[[0, 1]], base=0, channel_multiplier=1).then_inc(masks, 1)
            nc.gpsimd.memset(expand[:, :], 0.0).then_inc(masks, 1)
            nc.gpsimd.memset(ident_bf[:, :], 0.0).then_inc(masks, 1)
            pool.wait_ge(masks, 4)
            nc.gpsimd.affine_select(out=ident[:, :], in_=ident[:, :], compare_op=ALU.not_equal, fill=1.0,
                                    base=0, pattern=[[-1, P]], channel_multiplier=1).then_inc(masks, 1)
            nc.gpsimd.affine_select(out=expand[:, 0:RZ + NE], in_=expand[:, 0:RZ + NE], compare_op=ALU.not_equal,
                                    fill=1.0, base=0, pattern=[[-1, RZ + NE]], channel_multiplier=1
                                    ).then_inc(masks, 1)
            nc.gpsimd.affine_select(out=ident_bf[:, :], in_=ident_bf[:, :], compare_op=ALU.not_equal, fill=1.0,
                                    base=0, pattern=[[-1, P]], channel_multiplier=1).then_inc(masks, 1)
            pool.dma_start(id_sb[0:1, :], id1.rearrange("(o n) -> o n", o=1)).then_inc(id1_in, 16)
            gather_a0(pool, range(NB // 2, NB), a0_second)

            def gather_layer1(batches):
                for b in batches:
                    adapter = pool.value_load(id_sb[0:1, b:b + 1], min_val=0, max_val=NA1 - 1)
                    pool.dma_start(rows[b * RK:(b + 1) * RK, :],
                                   A1[bass.ds(adapter, 1)].rearrange("a r d -> (a r) d")).then_inc(a1rows_in, 16)
                    pool.dma_start(b1_in[:, b, :], b1_v[bass.ds(adapter, 1)].rearrange("a p c -> p (a c)")
                                   ).then_inc(b1_loaded, 16)

            def fill_bt(b, s):
                wait_from(pool, bxt_done, b - 1)
                nc.gpsimd.tensor_copy(bt_slot[:, s, :, :], bt[:, :, b, :].bitcast(F32)).then_inc(bt_filled, 1)

            pool.wait_ge(bt_ready, 2)
            fill_bt(0, 0)
            fill_bt(1, 1)
            pool.wait_ge(id1_in, 16)
            gather_layer1(range(0, 5))
            fill_bt(2, 0)
            fill_bt(3, 1)
            gather_layer1(range(5, NB))
            with pool.Fori(2, NB // 2) as q:
                fill_bt(q * 2, 0)
                fill_bt(q * 2 + 1, 1)
            pool.wait_ge(b1_loaded, 16 * NB)
            nc.gpsimd.tensor_copy(b1_k.rearrange("p k (b r) -> p k b r", b=NB),
                                  b1_in.rearrange("p b (k r) -> p k b r", k=KC)).then_inc(b1_ordered, 1)
            pool.wait_ge(amax_ready, 2)
            nc.gpsimd.partition_all_reduce(gmax[:, :], amax[:, :], P, bass.bass_isa.ReduceOp.max).then_inc(gmax_ready, 1)
            pool.wait_ge(raw_ready, 1)
            nc.gpsimd.tensor_tensor(a1_t[:, :, :, RK:2 * RK].rearrange("p b k r -> p k b r"),
                                    raw_a1.rearrange("p (k b r) -> p k b r", k=KC, b=NB),
                                    a1_t[:, :, :, 0:RK].bitcast(F32).rearrange("p b k r -> p k b r"),
                                    ALU.subtract).then_inc(lo_ready, 1)
            pool.wait_ge(raw_ready, 2)
            nc.gpsimd.tensor_tensor(b1_lo, raw_b1, b1_hi.bitcast(F32), ALU.subtract).then_inc(lo_ready, 1)

            def fill_a1(b):
                wait_from(pool, h_done, b * 2)
                nc.gpsimd.tensor_copy(a1_b, a1_t[:, bass.ds(b, 1), :, :].bitcast(F32).rearrange("p o k r -> p k o r"
                                      ).to_broadcast([P, KC, 3, HR])).then_inc(a1b_ready, 1)

            pool.wait_ge(lo_ready, 1)
            pool.wait_ge(bxt_done, NB)
            fill_a1(0)

            def low_of_u(i):
                pool.wait_ge(u_copied, i + 1)
                cols = bass.ds(i * P, P)
                nc.gpsimd.tensor_tensor(u_lo[:, cols], u_raw[:, cols], u_hi[:, cols].bitcast(F32),
                                        ALU.subtract).then_inc(u_split, 1)

            def fill_slot(b, j):
                wait_from(pool, slot_used, b * 2 + (j - 1))
                nc.gpsimd.tensor_copy(u_slot[:, j, :], u_tok[:, b, j, :]).then_inc(slot_ready, 1)

            with pool.Fori(0, KC - 2) as i:
                low_of_u(i)
            pool.wait_ge(u_ready, 1)
            fill_slot(0, 0)
            low_of_u(KC - 2)
            low_of_u(KC - 1)

            def step(t, b, j):
                go = Parts(t)
                if go.prev2:
                    pool.wait_ge(x1_copied, t - 1)
                    for half, cols in enumerate(HALVES):
                        pool.wait_ge(scaled_ready, (t - 2) * 2 + (1 + half))
                        nc.gpsimd.tensor_tensor(out_slot[j][:, cols], scaled[:, cols], out_slot[j][:, cols],
                                                ALU.add).then_inc(out_ready, 1)
                if not isinstance(t, int) or t + 2 < NT:
                    fill_slot(b + 1, j)
                    if j:
                        fill_a1(b + 1)

            fill_slot(0, 1)
            step(0, 0, 0)
            step(1, 0, 1)
            with pool.Fori(1, NB - 1) as b:
                step(b * 2, b, 0)
                step(b * 2 + 1, b, 1)
            for t in range(NT - 2, NT + 1):
                step(t, t // 2, t % 2)

        @block.scalar
        def _(act):
            act.dma_start(id_bc[:, :], id0.rearrange("(o n) -> o n", o=1).to_broadcast([P, NB])).then_inc(ids_in, 16)
            act.dma_start(w0_head, W0[0:NE, :]).then_inc(head_in, 16)
            with nc.allow_non_contiguous_dma(reason="small"):
                act.dma_start(m1[:, :, 0:RZ], Affn.rearrange("(p k) r -> p k r", p=P)).then_inc(affn_in, 16)
            act.wait_ge(chain, 3)
            nc.scalar.copy(p_b[:, :, NC:NR], e16[0:2 * RK, :].unsqueeze(1).to_broadcast([2 * RK, NB, RK])
                           ).then_inc(p_through, 1)
            with nc.allow_non_contiguous_dma(reason="small"):
                act.wait_ge(masks, 4)
                act.dma_start(expand[0:RZ, RZ + NE:NC], Lm.rearrange("e r -> r e")).then_inc(lt_in, 16)
                act.dma_start(split_in[0:RZ, :], Bmat[:, :]).then_inc(split_loaded, 16)
                act.dma_start(split_in[RZ:RZ + 1, :], b0.rearrange("(o n) -> o n", o=1)).then_inc(split_loaded, 16)
                act.dma_start(split_in[RZ + 1:RZ + 2, :], bb.rearrange("(o n) -> o n", o=1)).then_inc(split_loaded, 16)
                act.dma_start(l_bc[:, :, :].rearrange("p e r -> p (e r)"),
                              Lm.rearrange("(o e) r -> o (e r)", o=1).to_broadcast([P, NE * RZ])).then_inc(bc_in, 16)
                act.dma_start(b0_bc[:, :], b0[0:NE].rearrange("(o e) -> o e", o=1).to_broadcast([P, NE])
                              ).then_inc(bc_in, 16)
            for i in range(2):
                act.wait_ge(bt_done, i + 1)
                nc.scalar.copy(bt[:, i * KC // 2:(i + 1) * KC // 2, :, 0:RK],
                               pDE[i][:, :].rearrange("p (k b r) -> p k b r", b=NB, r=RK)).then_inc(bt_high, 1)

            def prepass(q):
                for i in range(2):
                    b = q * 2 + i
                    for j in range(2):
                        act.wait_ge(xt_done, b * 2 + (j + 1))
                        wait_from(act, bxt_done, b - 1)
                        nc.scalar.copy(xt_hi[i][:, :, j * P:(j + 1) * P], pAB3[j]).then_inc(xt_high, 1)
                    act.wait_ge(wbt_done, b + 1)
                    nc.scalar.copy(wb_hi[:, :, bass.ds(b * P, P)], pC3).then_inc(wb_high, 1)
                    if not isinstance(b, int) or b >= 1:
                        copy_bx(b - 1, 1 - i)
                    if not isinstance(b, int) or b >= 2:
                        copy_z(b - 2)

            def copy_bx(b, i):
                act.wait_ge(bxt_done, b + 1)
                wait_from(act, z_done, b - 1)
                nc.scalar.copy(bx_t[:, i, :], pD[0:2 * RK, 0:2 * P]).then_inc(bxt_copied, 1)

            def copy_z(b):
                act.wait_ge(z_done, b + 1)
                nc.scalar.copy(z_sb[:, :, bass.ds(b, 1), :].rearrange("p j o c -> p j (o c)"),
                               pE[:, 0:2 * NR].rearrange("p (j c) -> p j c", j=2)).then_inc(z_copied, 1)

            prepass(0)
            with act.Fori(1, NB // 2) as q:
                prepass(q)

            def copy_w0t(q, s):
                act.wait_ge(w0t_done, q * 2 + (s + 1))
                wait_from(act, u_done, q * 2 + (s - 1))
                nc.scalar.copy(w0t_raw[s], pAB[s][:, :]).then_inc(w0t_copied, 1)

            def copy_u(q, s):
                act.wait_ge(u_done, q * 2 + (s + 1))
                cols = bass.ds(q * 2 * P + s * P, P)
                nc.scalar.copy(u_hi[:, cols], pDE[s][:, 0:P])
                nc.scalar.copy(u_raw[:, cols], pDE[s][:, 0:P]).then_inc(u_copied, 1)

            copy_w0t(0, 0)
            copy_z(NB - 2)
            copy_bx(NB - 1, 1)
            copy_w0t(0, 1)
            copy_z(NB - 1)
            copy_u(0, 0)
            act.wait_ge(e1_in, 1)
            nc.scalar.activation(prob[:, :, :], logit[:, :, :], ACT.Exp).then_inc(e1_out, 1)
            act.wait_ge(a1t_done, 1)
            act.wait_ge(const_rows, 16 * 7)
            a1_src = pC[:, :].rearrange("p (k b r) -> p k b r", k=KC, b=NB)
            nc.scalar.copy(a1_t[:, :, :, 0:RK].rearrange("p b k r -> p k b r"), a1_src)
            nc.scalar.copy(raw_a1, pC[:, :]).then_inc(raw_ready, 1)
            copy_w0t(1, 0)
            copy_u(0, 1)
            act.wait_ge(e2_in, 1)
            nc.scalar.activation(gate[:, :, :], gate[:, :, :], ACT.Exp, scale=-2.0).then_inc(e2_out, 1)
            copy_w0t(1, 1)
            act.wait_ge(b1t_done, 1)
            nc.scalar.copy(b1_hi.rearrange("m (p k) -> m k p", k=KC), pC3)
            nc.scalar.copy(raw_b1.rearrange("m (p k) -> m k p", k=KC), pC3).then_inc(raw_ready, 1)
            with act.Fori(2, KC // 2) as q:
                copy_u(q - 1, 0)
                copy_w0t(q, 0)
                copy_u(q - 1, 1)
                copy_w0t(q, 1)
            copy_u(KC // 2 - 1, 0)
            copy_u(KC // 2 - 1, 1)

            def copy_w8(i):
                act.wait_ge(w8t_done, i + 1)
                nc.scalar.copy(w8_t[:, :, i * P:(i + 1) * P],
                               pABh[i % 4].rearrange("p (k c) -> p k c", k=KC)).then_inc(w8_act, 1)

            def copy_ut(t):
                act.wait_ge(slot_used, t + 1)
                wait_from(act, x1mm_done, t * 2)
                nc.scalar.copy(ut[:, :], pE[0:U1, 0:P]).then_inc(ut_ready, 1)

            def high_of_x1(t, half):
                act.wait_ge(x1t_done, t * 2 + (1 + half))
                chunks = slice(half * KC // 2, (half + 1) * KC // 2)
                nc.scalar.copy(x1t_hi[:, chunks, :], pC3[:, chunks, :]).then_inc(hi_ready, 1)

            copy_ut(0)
            copy_w8(1)
            copy_w8(3)
            high_of_x1(0, 0)
            copy_w8(5)
            copy_w8(7)
            high_of_x1(0, 1)

            def step(t, b, j):
                go = Parts(t)
                if go.prev:
                    wait_from(act, at_done, (t - 1) * 2)
                    for half, cols in enumerate(HALVES):
                        act.wait_ge(quant_ready, (t - 1) * 2 + (1 + half))
                        nc.scalar.activation(a_bf[:, cols], quant[:, cols], ACT.Copy, bias=-MAGIC).then_inc(abf_ready, 1)
                if go.next:
                    copy_ut(t + 1)
                if go.cur:
                    act.wait_ge(h_summed, t + 1)
                    wait_from(act, r_done, t)
                    nc.scalar.copy(ht[0:3 * HR, :], h_sum[:, :]).then_inc(h_rounded, 1)
                if go.prev:
                    wait_from(act, acc_done, (t - 1) * 2)
                    for half in range(2):
                        act.wait_ge(at_done, (t - 1) * 2 + (1 + half))
                        nc.scalar.copy(w8_bf[:, 1, HALVES[half]], go.a_t_bank[half][:, 0:HALF]).then_inc(at_ready, 1)
                if go.next:
                    high_of_x1(t + 1, 0)
                    high_of_x1(t + 1, 1)
                if go.cur:
                    wait_from(act, stored[j], b * 16)
                    nc.scalar.copy(out_slot[j], x1[:, j, :]).then_inc(x1_copied, 1)

            main_steps(act, step)

        @block.vector
        def _(dve):
            nc.vector.memset(ht[3 * HR:U2, :].bitcast(F32), 1.0).then_inc(ones_set, 1)
            links = [0]

            def link(instruction):
                links[0] += 1
                instruction.then_inc(chain, 1)
                dve.wait_ge(chain, links[0])

            dve.wait_ge(masks, 7)
            link(nc.vector.tensor_scalar(part[:, :], part[:, :], 4, None, ALU.logical_shift_right))
            link(nc.vector.tensor_copy(block_f[:, :], part[:, :]))
            link(nc.vector.tensor_reduce(e16[:, :], ident[:, :].rearrange("p (b r) -> p r b", b=NB), AX.X, ALU.add))
            dve.wait_ge(ids_in, 16)
            link(nc.vector.tensor_copy(id_f[:, :], id_bc[:, :]))
            link(nc.vector.tensor_scalar(onehot[:, :], id_f[:, :], block_f[:, :], None, ALU.is_equal))
            nc.vector.tensor_tensor(pick[:, :, :], onehot[:, :].unsqueeze(2).to_broadcast([P, NB, RK]),
                                    e16[:, :].unsqueeze(1).to_broadcast([P, NB, RK]), ALU.mult).then_inc(pick_ready, 1)
            for i in range(2):
                dve.wait_ge(bt_high, i + 1)
                chunks = slice(i * KC // 2, (i + 1) * KC // 2)
                nc.vector.tensor_tensor(bt[:, chunks, :, RK:2 * RK],
                                        pDE[i][:, :].rearrange("p (k b r) -> p k b r", b=NB, r=RK),
                                        bt[:, chunks, :, 0:RK].bitcast(F32), ALU.subtract).then_inc(bt_ready, 1)
            def split_x(b, i, j):
                dve.wait_ge(xt_high, b * 2 + (j + 1))
                nc.vector.tensor_tensor(xt_lo[i][:, :, j * P:(j + 1) * P], pAB3[j],
                                        xt_hi[i][:, :, j * P:(j + 1) * P].bitcast(F32), ALU.subtract).then_inc(xt_split, 1)

            def split_wb(b):
                dve.wait_ge(wb_high, b + 1)
                nc.vector.tensor_tensor(wb_lo[:, :, bass.ds(b * P, P)], pC3,
                                        wb_hi[:, :, bass.ds(b * P, P)].bitcast(F32), ALU.subtract).then_inc(wb_split, 1)

            split_x(0, 0, 0)
            split_x(0, 0, 1)
            split_wb(0)
            dve.wait_ge(p_step, 1)
            nc.vector.tensor_copy(m1[:, :, RZ:RZ + NE], pE[:, 0:KC * NE].rearrange("p (k e) -> p k e", k=KC)
                                  ).then_inc(p_copied, 1)
            split_x(1, 1, 0)
            dve.wait_ge(a0_first, 16 * NB // 2)
            dve.wait_ge(a0_second, 16 * NB // 2)
            nc.vector.tensor_copy(a0_k.rearrange("p k (b r) -> p k b r", b=NB),
                                  a0_in.rearrange("p b (k r) -> p k b r", k=KC)).then_inc(a0_ordered, 1)
            split_x(1, 1, 1)
            split_wb(1)
            dve.wait_ge(p_step, 2)
            nc.vector.tensor_copy(p_t[:, :, :, :], pE[0:RZ + NE, 0:P].rearrange("m (b o r) -> m b o r", b=NB, o=1
                                  ).to_broadcast([RZ + NE, NB, 2, RK])).then_inc(p_copied, 1)
            dve.wait_ge(p_step, 3)
            nc.vector.tensor_copy(p_b[:, :, 0:NC], pE[0:2 * RK, 0:NB * NC].rearrange("p (b c) -> p b c", b=NB)
                                  ).then_inc(p_copied, 1)
            dve.wait_ge(split_loaded, 48)
            link(nc.vector.tensor_copy(split_hi, split_in))
            nc.vector.tensor_tensor(split_lo, split_in, split_hi.bitcast(F32), ALU.subtract).then_inc(split_done, 1)
            with dve.Fori(1, NB // 2) as q:
                for i in range(2):
                    split_x(q * 2 + i, i, 0)
                    split_x(q * 2 + i, i, 1)
                    split_wb(q * 2 + i)
            dve.wait_ge(z_copied, NB)
            dve.wait_ge(bc_in, 32)
            hs, ds_ = z_sb[:, 1, :, RZ:RZ + NE], z_sb[:, 1, :, RZ + NE:NC]
            link(nc.vector.tensor_tensor(hs, hs, b0_bc[:, :].unsqueeze(1).to_broadcast([P, NB, NE]), ALU.add))
            nc.vector.tensor_reduce(amax[:, 0:1], hs, AX.XY, ALU.max, apply_absolute_value=True).then_inc(amax_ready, 1)
            nc.vector.tensor_reduce(amax[:, 1:2], ds_, AX.XY, ALU.max, apply_absolute_value=True).then_inc(amax_ready, 1)
            dve.wait_ge(gmax_ready, 1)
            link(nc.vector.tensor_scalar(gmax[:, :], gmax[:, :], 1e-6, 2.0, ALU.max, ALU.mult))
            link(nc.vector.reciprocal(ginv[:, :], gmax[:, :]))
            link(nc.vector.tensor_scalar(logit[:, :, :], ds_, ginv[:, 1:2], None, ALU.mult))
            link(nc.vector.scalar_tensor_tensor(logit[:, :, :], hs, ginv[:, 0:1], logit[:, :, :], ALU.mult, ALU.add))
            link(nc.vector.tensor_reduce(stat[:, :], logit[:, :, :], AX.X, ALU.max))
            nc.vector.tensor_tensor(logit[:, :, :], logit[:, :, :], stat[:, :].unsqueeze(2).to_broadcast([P, NB, NE]),
                                    ALU.subtract).then_inc(e1_in, 1)
            dve.wait_ge(e1_out, 1)
            link(nc.vector.tensor_reduce(stat[:, :], prob[:, :, :], AX.X, ALU.add))
            link(nc.vector.reciprocal(stat[:, :], stat[:, :]))
            link(nc.vector.tensor_tensor(prob[:, :, :], prob[:, :, :],
                                         stat[:, :].unsqueeze(2).to_broadcast([P, NB, NE]), ALU.mult))
            for b in range(NB):
                last = nc.vector.max(top8[:, b, :], prob[:, b, :])
            link(last)
            nc.vector.tensor_tensor(gate[:, :, :], prob[:, :, :], top8[:, :, 1:2].to_broadcast([P, NB, NE]),
                                    ALU.subtract).then_inc(e2_in, 1)
            dve.wait_ge(e2_out, 1)
            link(nc.vector.tensor_scalar(gate[:, :, :], gate[:, :, :], 1.0, None, ALU.add))
            link(nc.vector.reciprocal(gate[:, :, :], gate[:, :, :]))
            link(nc.vector.tensor_tensor(gate[:, :, :], gate[:, :, :], prob[:, :, :], ALU.mult))
            link(nc.vector.tensor_reduce(stat[:, :], gate[:, :, :], AX.X, ALU.add))
            link(nc.vector.tensor_scalar(stat[:, :], stat[:, :], 1e-9, None, ALU.add))
            link(nc.vector.reciprocal(stat[:, :], stat[:, :]))
            link(nc.vector.tensor_tensor(gate[:, :, :], gate[:, :, :],
                                         stat[:, :].unsqueeze(2).to_broadcast([P, NB, NE]), ALU.mult))
            for b in range(NB):
                last = nc.vector.tensor_tensor(mixprod[:, b, :, :], gate[:, b, :].unsqueeze(1).to_broadcast([P, RZ, NE]),
                                               l_bc[:, :, :].rearrange("p e r -> p r e"), ALU.mult)
            link(last)
            link(nc.vector.tensor_reduce(pmix[:, :, :], mixprod[:, :, :, :], AX.X, ALU.add))
            nc.vector.memset(u_tok[:, :, :, 2 * NU:U1], 1.0).then_inc(ones_set, 1)
            for j in range(2):
                link(nc.vector.scalar_tensor_tensor(u_tok[:, :, j, RK:NU], z_sb[:, j, :, 0:RZ], 0.5, pmix[:, :, :],
                                                    ALU.mult, ALU.mult))
                link(nc.vector.tensor_copy(u_tok[:, :, j, 0:RK], z_sb[:, j, :, NC:NR]))
                link(nc.vector.tensor_copy(u_round[:, :, j, :], u_tok[:, :, j, 0:NU]))
                last = nc.vector.tensor_tensor(u_tok[:, :, j, NU:2 * NU], u_tok[:, :, j, 0:NU],
                                               u_round[:, :, j, :].bitcast(F32), ALU.subtract)
                if j == 0:
                    link(last)
            last.then_inc(u_ready, 1)
            dve.wait_ge(w8_in, 16)
            dve.wait_ge(b1_ordered, 1)
            dve.wait_ge(u_ready, 1)
            for i in range(KC):
                nc.vector.tensor_copy(w8_tile[i], w8_in8[:, i, :].bitcast(I8)).then_inc(w8_conv, 1)

            def copy_w8(i):
                dve.wait_ge(w8t_done, i + 1)
                nc.vector.tensor_copy(w8_t[:, :, i * P:(i + 1) * P],
                                      pABh[i % 4].rearrange("p (k c) -> p k c", k=KC)).then_inc(w8_dve, 1)

            def add_x(t, slot, half):
                dve.wait_ge(x1mm_done, t * 2 + (1 + half))
                cols = HALVES[half]
                nc.vector.tensor_tensor(x1[:, slot, cols], pC[:, cols], x_ring[:, slot, cols], ALU.add
                                        ).then_inc(x1_ready, 1)

            def quantise(half):
                nc.vector.tensor_scalar(quant[:, HALVES[half]], pA[:, HALVES[half]], a_inv[:, :], MAGIC,
                                        ALU.mult, ALU.add).then_inc(quant_ready, 1)

            def low_of_x1(t, half):
                dve.wait_ge(hi_ready, t * 2 + (1 + half))
                chunks = slice(half * KC // 2, (half + 1) * KC // 2)
                nc.vector.tensor_tensor(x1t_lo[:, chunks, :], pC3[:, chunks, :], x1t_hi[:, chunks, :].bitcast(F32),
                                        ALU.subtract).then_inc(x1lo_ready, 1)

            def step(t, b, j):
                go = Parts(t)
                nj = 1 - j
                if go.cur:
                    dve.wait_ge(h_done, t + 1)
                    nc.vector.tensor_reduce(h_sum[:, :], pD[0:3 * HR, 0:2 * P].rearrange("m (c t) -> m t c", c=2),
                                            AX.X, ALU.add).then_inc(h_summed, 1)
                    dve.wait_ge(h_rounded, t + 1)
                    low = slice(2 * HR, 3 * HR)
                    nc.vector.tensor_tensor(ht[low, :], h_sum[low, :], ht[low, :].bitcast(F32),
                                            ALU.subtract).then_inc(ht_ready, 1)
                if go.prev2:
                    wait_from(dve, out_ready, (t - 2) * 2)
                    if isinstance(t, int) and t == NT + 1:
                        dve.wait_ge(x1_copied, NT)
                        for i, cols in enumerate(ENDING):
                            dve.wait_ge(acc_done, (NT - 1) * 2 + 1 + i)
                            nc.vector.scalar_tensor_tensor(scaled[:, cols], ending[i], a_scale[:, j:j + 1], ws_bc[:, cols],
                                                           ALU.mult, ALU.mult).then_inc(scaled_ready, 1)
                            dve.wait_ge(scaled_ready, (NT - 1) * 2 + 1 + i)
                            nc.vector.tensor_tensor(out_slot[j][:, cols], scaled[:, cols], out_slot[j][:, cols],
                                                    ALU.add).then_inc(out_ready, 1)
                    else:
                        for half, cols in enumerate(HALVES):
                            dve.wait_ge(acc_done, (t - 2) * 2 + (1 + half))
                            nc.vector.scalar_tensor_tensor(scaled[:, cols], pB[:, cols], a_scale[:, j:j + 1],
                                                           ws_bc[:, cols], ALU.mult, ALU.mult).then_inc(scaled_ready, 1)
                if go.next:
                    dve.wait_ge(xm_in[nj], (b + (1 if j else 0)) * 16 + 16)
                    wait_from(dve, x1_copied, t)
                    add_x(t + 1, nj, 0)
                    add_x(t + 1, nj, 1)
                if go.cur:
                    dve.wait_ge(r0_done, t + 1)
                    nc.vector.tensor_reduce(mag2[:, 0:1], pA[:, 0:HALF], AX.X, ALU.max, apply_absolute_value=True
                                            ).then_inc(mag_ready, 1)
                    dve.wait_ge(r_done, t + 1)
                    nc.vector.tensor_reduce(mag2[:, 1:2], pA[:, HALF:D], AX.X, ALU.max, apply_absolute_value=True
                                            ).then_inc(mag_ready, 1)
                    dve.wait_ge(mag_ready, t * 2 + 2)
                    nc.vector.tensor_tensor(mag[:, :], mag2[:, 0:1], mag2[:, 1:2], ALU.max).then_inc(mag1_ready, 1)
                if go.next:
                    low_of_x1(t + 1, 0)
                if go.cur:
                    dve.wait_ge(mag1_ready, t + 1)
                    nc.vector.tensor_scalar(a_scale[:, j:j + 1], mag[:, :], 1.0 / QMAX, TINY, ALU.mult, ALU.max
                                            ).then_inc(scale_ready, 1)
                    dve.wait_ge(scale_ready, t + 1)
                    nc.vector.reciprocal(a_inv[:, :], a_scale[:, j:j + 1]).then_inc(inv_ready, 1)
                    dve.wait_ge(inv_ready, t + 1)
                    wait_from(dve, abf_ready, t * 2)
                    quantise(0)
                if go.next:
                    low_of_x1(t + 1, 1)
                if go.cur:
                    quantise(1)

            copy_w8(0)
            copy_w8(2)
            dve.wait_ge(w0t_done, KC)
            dve.wait_ge(xm_in[0], 16)
            add_x(0, 0, 0)
            copy_w8(4)
            low_of_x1(0, 0)
            copy_w8(6)
            add_x(0, 0, 1)
            low_of_x1(0, 1)
            dve.wait_ge(ws_in, 16)
            main_steps(dve, step)

        @block.tensor
        def _(pe):
            pe.wait_ge(masks, 5)
            for _ in range(WARM_UP):
                nc.tensor.transpose(pC3[:, 0, :], ident[:, :], ident[:, :])
            pe.wait_ge(b_in, 16)
            pe.wait_ge(pick_ready, 1)
            pick_m = pick[:, :, :].rearrange("p b r -> p (b r)")
            for k in range(KC):
                last = nc.tensor.matmul(pDE[k // 4][:, k % 4 * P:(k % 4 + 1) * P], rows[:, k * P:(k + 1) * P], pick_m,
                                        start=True, stop=True)
                if k % 4 == 3:
                    last.then_inc(bt_done, 1)

            def transpose_x(b, i, j):
                s = 2 * i + j
                pe.wait_ge(x_in[s], (b - i) * 8 + 16)
                wait_from(pe, xt_split, b * 2 + (j - 1))
                for k in range(KC):
                    last = nc.tensor.transpose(pAB3[j][:, k, :], x_ring[:, s, k * P:(k + 1) * P], ident[:, :])
                last.then_inc(xt_done, 1)

            def transpose_wb(b, i):
                pe.wait_ge(wb_in[i], (b - i) * 8 + 16)
                wait_from(pe, wb_split, b)
                for k in range(KC):
                    last = nc.tensor.transpose(pC3[:, k, :], wb_ring[:, i, k * P:(k + 1) * P], ident[:, :])
                last.then_inc(wbt_done, 1)

            def project(b, i):
                pe.wait_ge(bt_filled, b + 1)
                pe.wait_ge(xt_split, b * 2 + 2)
                wait_from(pe, bxt_copied, b)
                for k in range(KC):
                    nc.tensor.matmul(pD[0:2 * RK, 0:2 * P], bt_slot[:, i, k, :], xt_hi[i][:, k, :],
                                     start=(k == 0), stop=False)
                    last = nc.tensor.matmul(pD[0:RK, 0:2 * P], bt_slot[:, i, k, 0:RK], xt_lo[i][:, k, :],
                                            start=False, stop=(k == KC - 1))
                last.then_inc(bxt_done, 1)

            def route(b, i):
                pe.wait_ge(bxt_copied, b + 1)
                pe.wait_ge(p_copied, 3)
                pe.wait_ge(p_through, 1)
                wait_from(pe, z_copied, b)
                for j in range(2):
                    last = nc.tensor.matmul(pE[:, j * NR:(j + 1) * NR], bx_t[:, i, j * P:(j + 1) * P],
                                            p_b[:, bass.ds(b, 1), :].rearrange("p o c -> p (o c)"),
                                            start=True, stop=True)
                last.then_inc(z_done, 1)

            def prepass(q):
                for i in range(2):
                    b = q * 2 + i
                    transpose_x(b, i, 0)
                    transpose_x(b, i, 1)
                    if not isinstance(b, int) or b >= 2:
                        route(b - 2, i)
                    transpose_wb(b, i)
                    if isinstance(b, int) and b == 0:
                        pe.wait_ge(bt_ready, 2)
                        head_of_w0()
                    if not isinstance(b, int) or b >= 1:
                        project(b - 1, 1 - i)
                    if isinstance(b, int) and b == 1:
                        head_by_a()
                        to_p_b()

            def head_of_w0():
                pe.wait_ge(head_in, 16)
                for k in range(KC):
                    last = nc.tensor.transpose(pE[:, k * NE:(k + 1) * NE], w0_head[:, k:D:KC], ident[0:NE, 0:NE])
                last.then_inc(p_step, 1)

            def head_by_a():
                pe.wait_ge(p_copied, 1)
                pe.wait_ge(affn_in, 16)
                pe.wait_ge(a0_ordered, 1)
                for k in range(KC):
                    last = nc.tensor.matmul(pE[0:RZ + NE, 0:P], m1[:, k, :], a0_k[:, k, :], start=(k == 0), stop=(k == KC - 1))
                last.then_inc(p_step, 1)

            def to_p_b():
                pe.wait_ge(p_copied, 2)
                pe.wait_ge(lt_in, 16)
                for b in range(NB):
                    last = nc.tensor.matmul(pE[0:2 * RK, b * NC:(b + 1) * NC],
                                            p_t[:, b, :, :].rearrange("m h r -> m (h r)"), expand[:, :],
                                            start=True, stop=True)
                last.then_inc(p_step, 1)

            prepass(0)
            with pe.Fori(1, NB // 2) as q:
                prepass(q)

            def transpose_w0(q, s):
                pe.wait_ge(w0_in[s], q * 16 + 16)
                wait_from(pe, w0t_copied, q * 2 + (s - 1))
                for k in range(KC):
                    last = nc.tensor.transpose(pAB3[s][:, k, :], w0_ring[:, s, k:D:KC], ident[:, :])
                last.then_inc(w0t_done, 1)

            def apply_w0(q, s):
                pe.wait_ge(w0t_copied, q * 2 + (s + 1))
                wait_from(pe, u_copied, q * 2 + (s - 1))
                for k in range(KC):
                    last = nc.tensor.matmul(pDE[s][:, 0:P], a0_k[:, k, :], w0t_raw[s][:, k * P:(k + 1) * P],
                                            start=(k == 0), stop=(k == KC - 1))
                last.then_inc(u_done, 1)

            pe.wait_ge(xt_split, NT - 1)
            transpose_w0(0, 0)
            route(NB - 2, 0)
            project(NB - 1, 1)
            transpose_w0(0, 1)
            route(NB - 1, 1)
            pe.wait_ge(bxt_copied, NB)
            apply_w0(0, 0)
            pe.wait_ge(a1rows_in, 16 * NB)
            pe.wait_ge(wb_split, KC)
            for k in range(KC):
                last = nc.tensor.transpose(pC3[:, k, :], rows[:, k * P:(k + 1) * P], ident[:, :])
            last.then_inc(a1t_done, 1)
            transpose_w0(1, 0)
            pe.wait_ge(z_copied, NB)
            apply_w0(0, 1)
            transpose_w0(1, 1)
            pe.wait_ge(b1_ordered, 1)
            pe.wait_ge(raw_ready, 1)
            for k in range(KC):
                last = nc.tensor.transpose(pC3[:, k, :], b1_k[:, k, :], ident[:, :])
            last.then_inc(b1t_done, 1)
            with pe.Fori(2, KC // 2) as q:
                apply_w0(q - 1, 0)
                transpose_w0(q, 0)
                apply_w0(q - 1, 1)
                transpose_w0(q, 1)
            apply_w0(KC // 2 - 1, 0)
            apply_w0(KC // 2 - 1, 1)

            def transpose_w8(i):
                pe.wait_ge(w8_conv, i + 1)
                wait_from(pe, (w8_dve, w8_act)[i % 2], (i - 2) // 2)
                for k in range(KC):
                    last = nc.tensor.transpose(pABh[i % 4][:, k * P:(k + 1) * P], w8_tile[i][:, k * P:(k + 1) * P],
                                               ident_bf[:, :])
                last.then_inc(w8t_done, 1)

            def transpose_update(t, slot):
                pe.wait_ge(slot_ready, t + 1)
                wait_from(pe, ut_ready, t)
                nc.tensor.transpose(pE[0:U1, 0:P], u_slot[:, slot, :], ident[:, :]).then_inc(slot_used, 1)

            def update(half):
                cols = HALVES[half]
                nc.tensor.matmul(pC[:, cols], ut[:, :], upd_hi[:, cols], start=True, stop=False)
                nc.tensor.matmul(pC[:, cols], ut[0:NU, :], upd_lo[:, cols], start=False, stop=True
                                 ).then_inc(x1mm_done, 1)

            def transpose_x1(t, slot, half):
                pe.wait_ge(x1_ready, t * 2 + (1 + half))
                for k in HALF_CHUNKS[half]:
                    last = nc.tensor.transpose(pC3[:, k, :], x1[:, slot, k * P:(k + 1) * P], ident[:, :])
                last.then_inc(x1t_done, 1)

            pe.wait_ge(ones_set, 2)
            pe.wait_ge(const_rows, 16 * 7)
            transpose_w8(0)
            transpose_w8(1)
            pe.wait_ge(u_copied, KC)
            transpose_update(0, 0)
            transpose_w8(2)
            transpose_w8(3)
            pe.wait_ge(ut_ready, 1)
            pe.wait_ge(upd_first, 48)
            pe.wait_ge(raw_ready, 2)
            update(0)
            transpose_w8(4)
            transpose_w8(5)
            transpose_x1(0, 0, 0)
            transpose_w8(6)
            transpose_w8(7)
            pe.wait_ge(upd_in, 48)
            update(1)

            def step(t, b, j):
                go = Parts(t)
                nb = b + (1 if j else 0)
                if go.next:
                    transpose_update(t + 1, 1 - j)
                if isinstance(t, int) and t == 0:
                    pe.wait_ge(w8_dve, KC // 2 - 1)
                    pe.wait_ge(w8_act, KC // 2 - 1)
                if isinstance(t, int) and t == 1:
                    pe.wait_ge(w8_dve, KC // 2)
                    pe.wait_ge(w8_act, KC // 2)
                if go.cur:
                    pe.wait_ge(a1b_ready, b + 1)
                    wait_from(pe, h_summed, t)

                def product(half, chunks):
                    cols = HALVES[half]
                    for k in chunks:
                        nc.tensor.matmul(pA[:, cols], x1t_hi[:, k, :], wb_hi[:, k, cols], start=(k == 0), stop=False)
                        nc.tensor.matmul(pA[:, cols], x1t_hi[:, k, :], wb_lo[:, k, cols], start=False, stop=False)
                        nc.tensor.matmul(pA[:, cols], x1t_lo[:, k, :], wb_hi[:, k, cols], start=False, stop=False)

                def quant_read(half):
                    if not isinstance(t, int) or t > 0:
                        pe.wait_ge(quant_ready, (t - 1) * 2 + (1 + half))

                def lora(half):
                    cols = HALVES[half]
                    return nc.tensor.matmul(pA[:, cols], ht[:, :], lora_r[:, cols], start=False, stop=True)

                if go.cur:
                    for half in range(2):
                        pe.wait_ge(hi_ready, t * 2 + (1 + half))
                        pe.wait_ge(x1lo_ready, t * 2 + (1 + half))
                        for k in HALF_CHUNKS[half]:
                            last = nc.tensor.matmul(pD[0:3 * HR, 0:2 * P], a1_b[:, k, :, :].rearrange("p c r -> p (c r)"),
                                                    x1t_both[:, k, :], start=(k == 0), stop=(k == KC - 1))
                        if half == 1:
                            last.then_inc(h_done, 1)
                        quant_read(0)
                        if isinstance(t, int) and t == 0 and half == 0:
                            product(0, range(0, 2))
                            transpose_x1(0, 0, 1)
                            product(0, range(2, KC // 2))
                        else:
                            product(0, HALF_CHUNKS[half])
                if go.next:
                    pe.wait_ge(ut_ready, t + 2)
                    pe.wait_ge(upd_in, nb * 48 + 48)
                    wait_from(pe, x1lo_ready, (t + 1) * 2)
                    update(0)
                    update(1)
                if go.prev:
                    if not go.ends:
                        wait_from(pe, scaled_ready, (t - 1) * 2)
                    for half in range(2):
                        pe.wait_ge(abf_ready, (t - 1) * 2 + (1 + half))
                        for i, k in enumerate(HALF_CHUNKS[half]):
                            last = nc.tensor.transpose(go.a_t_bank[half][:, i * P:(i + 1) * P], a_bf[:, k * P:(k + 1) * P],
                                                       ident_bf[:, :])
                        last.then_inc(at_done, 1)
                if go.cur:
                    pe.wait_ge(ht_ready, t + 1)
                    pe.wait_ge(lora_in, (b + 1) * 16 * 6)
                    lora(0).then_inc(r0_done, 1)
                    quant_read(1)
                    product(1, range(KC))
                    lora(1).then_inc(r_done, 1)
                if go.next:
                    transpose_x1(t + 1, 1 - j, 0)
                    transpose_x1(t + 1, 1 - j, 1)
                if go.prev:
                    if go.ends:
                        pe.wait_ge(scaled_ready, (NT - 1) * 2)
                    for acc, cols in zip(ending, ENDING) if go.ends else ((pB[:, cols], cols) for cols in HALVES):
                        for half in range(2):
                            pe.wait_ge(at_ready, (t - 1) * 2 + (1 + half))
                            for k in HALF_CHUNKS[half]:
                                last = nc.tensor.matmul(acc, a_t[:, k, :], w8_t[:, k, cols],
                                                        start=(k == 0), stop=(k == KC - 1))
                        last.then_inc(acc_done, 1)

            main_steps(pe, step)


_INS = ['x', 'itok_B_3_7', 'itok_B_6_15', 'L0_cond_A', 'L0_cond_B', 'L0_ffn_W', 'L0_ffn_b', 'L0_ffn_A', 'L0_ffn_Bmat',
        'L0_ffn_LiMEs', 'L1_cond_base_weight', 'L1_cond_base_bias', 'L1_cond_lora_A_w', 'L1_cond_lora_B_w',
        'L1_ffn_weight', 'L1_ffn_weight_scale']


def kernel(**inputs):
    import numpy as _np
    import concourse.bacc as _bacc
    from concourse import mybir as _mybir
    from concourse.bass_utils import run_bass_kernel_spmd as _run

    nc = _bacc.Bacc("TRN2", target_bir_lowering=False, num_devices=1)
    arrays, args = {}, []
    for name in _INS:
        a = _np.ascontiguousarray(inputs[name])
        if a.dtype.itemsize == 1:
            a = a.view(_np.int32)
        arrays[f"in_{name}_dram"] = a
        args.append(nc.dram_tensor(f"in_{name}_dram", a.shape, _mybir.dt.from_np(a.dtype), kind="ExternalInput").ap())
    args.append(nc.dram_tensor("out_0_dram", (NB, 2 * P, D), F32, kind="ExternalOutput").ap())
    ffn_kernel(nc, *args)
    r = _run(nc, [arrays], core_ids=[0])
    return r.results[0]["out_0_dram"]
```
